# Optimizing a Trainium2 kernel written in Bass

```python
import numpy as np
import jax
import jax.numpy as jnp

def _softmax(x, axis=-1):
    return jax.nn.softmax(x, axis=axis)

def _gelu(x):
    return jax.nn.gelu(x, approximate=True)

def _silu(x):
    return jax.nn.silu(x)

def _sigmoid(x):
    return jax.nn.sigmoid(x)

def _layernorm(x, axis=-1, eps=1e-05):
    m = jnp.mean(x, axis=axis, keepdims=True)
    v = jnp.var(x, axis=axis, keepdims=True)
    return (x - m) / jnp.sqrt(v + eps)

def _scatter_add(tgt, idx, src, axis=0):
    return tgt.at[idx].add(src)

def _segment_sum(src, seg, n):
    return jax.ops.segment_sum(src, seg, n)
kernel_name = 'mk_flamingo_gated_d1_seqx_r4_774133'

def setup_inputs(seed: int=0):
    np.random.seed(seed)
    _w = jnp.asarray

    def _rec_inputs():
        import jax
        import jax.numpy as jnp
        _rk = jax.random.key(seed)
        x = 4.136e-05 + 0.9999 * jax.random.normal(jax.random.fold_in(_rk, 1), (4, 512, 512), jnp.float32)
        _lenS = 512 - jax.random.randint(jax.random.fold_in(_rk, 7), (4,), 0, max(1, 512 // 4) + 1, jnp.int32)
        _lenS2 = 512 - jax.random.randint(jax.random.fold_in(_rk, 8), (4,), 0, max(1, 512 // 4) + 1, jnp.int32)
        _ctx_1024P = jax.random.normal(jax.random.fold_in(_rk, 11), (4, 16, 256), jnp.float32)
        _ctx_1024c = jax.random.dirichlet(jax.random.fold_in(_rk, 511), 0.3 * jnp.ones((16,), jnp.float32), (4, 512))
        _ctx_1024t = jnp.einsum('bsk,bkd->bsd', _ctx_1024c, _ctx_1024P)
        _ctx_1024t = _ctx_1024t * jax.lax.rsqrt(jnp.mean(jnp.square(_ctx_1024t)) + 1e-12) * 0.953939
        ctx_1024 = -0.000292821 + 1.00034 * (_ctx_1024t + 0.3 * jax.random.normal(jax.random.fold_in(_rk, 611), (4, 512, 256), jnp.float32))
        _g = jax.random.normal(jax.random.fold_in(_rk, 9001), (2, 1), jnp.float32)
        _g = jnp.sign(_g) * jnp.maximum(jnp.abs(_g), 1.0) + (_g == 0) * 1.0
        g_xattn = _g[0]
        g_ffn = _g[1]
        return (x, ctx_1024, g_xattn, g_ffn)
    x, ctx_1024, g_xattn, g_ffn = _rec_inputs()

    def _L0_xattn_setup():
        import jax, jax.numpy as jnp
        import numpy as np
        import math
        B, L, DM = (2, 512, 256)
        DS, DC, EXP = (16, 4, 2)
        DI = EXP * DM
        DR = math.ceil(DM / 16)
        DT_MIN, DT_MAX, DT_FLOOR = (0.001, 0.1, 0.0001)

        def _ssm_forward(hidden_states, z, in_proj_w, conv_w, conv_b, x_proj_w, dt_proj_w, dt_proj_b, A_log, D):
            b = hidden_states.shape[0]
            x = jnp.einsum('ed,bld->bel', in_proj_w, hidden_states)
            xp = jnp.pad(x, ((0, 0), (0, 0), (DC - 1, 0)))
            xc = jax.lax.conv_general_dilated(xp, conv_w[:, None, :], window_strides=(1,), padding='VALID', dimension_numbers=('NCH', 'OIH', 'NCH'), feature_group_count=DI)
            u = jax.nn.silu(xc + conv_b[None, :, None])
            x_dbl = jnp.einsum('ke,bel->bkl', x_proj_w, u)
            dt_lo = x_dbl[:, :DR]
            Bm = x_dbl[:, DR:DR + DS]
            Cm = x_dbl[:, DR + DS:]
            delta = jax.nn.softplus(jnp.einsum('er,brl->bel', dt_proj_w, dt_lo) + dt_proj_b[None, :, None])
            A = -jnp.exp(A_log)

            def step(state, xs):
                d_t, B_t, C_t, u_t = xs
                dA = jnp.exp(d_t[..., None] * A)
                state = state * dA + (d_t * u_t)[..., None] * B_t[:, None, :]
                y_t = jnp.einsum('ben,bn->be', state, C_t)
                return (state, y_t)
            xs = (jnp.moveaxis(delta, -1, 0), jnp.moveaxis(Bm, -1, 0), jnp.moveaxis(Cm, -1, 0), jnp.moveaxis(u, -1, 0))
            state0 = jnp.zeros((b, DI, DS), delta.dtype)
            _, ys = jax.lax.scan(step, state0, xs)
            y = jnp.moveaxis(ys, 0, -1)
            y = y + D[None, :, None] * u
            y = y * jax.nn.silu(z)
            return jnp.swapaxes(y, 1, 2)
        key = jax.random.key(seed)
        ks = jax.random.split(key, 8)
        hidden_states = jax.random.normal(ks[0], (B, L, DM), jnp.float32)
        z = jax.random.normal(ks[1], (B, DI, L), jnp.float32)
        in_proj_w = jax.random.normal(ks[2], (DI, DM), jnp.float32) * DM ** (-0.5)
        conv_w = jax.random.normal(ks[3], (DI, DC), jnp.float32) * DC ** (-0.5)
        conv_b = jnp.zeros((DI,), jnp.float32)
        x_proj_w = jax.random.normal(ks[4], (DR + 2 * DS, DI), jnp.float32) * DI ** (-0.5)
        dt_std = DR ** (-0.5)
        dt_proj_w = jax.random.uniform(ks[5], (DI, DR), jnp.float32, -dt_std, dt_std)
        dt = jnp.exp(jax.random.uniform(ks[6], (DI,), jnp.float32) * (math.log(DT_MAX) - math.log(DT_MIN)) + math.log(DT_MIN))
        dt = jnp.clip(dt, DT_FLOOR)
        dt_proj_b = dt + jnp.log(-jnp.expm1(-dt))
        A_log = jnp.log(jnp.broadcast_to(jnp.arange(1, DS + 1, dtype=jnp.float32), (DI, DS)))
        D = jnp.ones((DI,), jnp.float32)
        return dict(hidden_states=hidden_states, z=z, in_proj_w=in_proj_w, conv_w=conv_w, conv_b=conv_b, x_proj_w=x_proj_w, dt_proj_w=dt_proj_w, dt_proj_b=dt_proj_b, A_log=A_log, D=D)
    _L0_xattn_all = _L0_xattn_setup()
    _L0_xattn_in = {k: v for k, v in _L0_xattn_all.items() if k in ('in_proj_w', 'conv_w', 'conv_b', 'x_proj_w', 'dt_proj_w', 'dt_proj_b', 'A_log', 'D')}
    del _L0_xattn_all

    def _L0_ffn_setup():
        import jax, jax.numpy as jnp
        import numpy as np
        NUM_EXPERTS = 8
        TOP_K = 2
        key = jax.random.key(seed)
        ks = jax.random.split(key, 7)
        B, S, H, I, E = (4, 512, 512, 512, NUM_EXPERTS)
        sc = 0.02
        return {'hidden_states': jax.random.normal(ks[0], (B, S, H), dtype=jnp.float32), 'gate_w': jax.random.normal(ks[1], (E, H), dtype=jnp.float32) * sc, 'gate_b': jax.random.normal(ks[2], (E,), dtype=jnp.float32) * sc, 'w1': jax.random.normal(ks[3], (E, 2 * I, H), dtype=jnp.float32) * sc, 'b1': jax.random.normal(ks[4], (E, 2 * I), dtype=jnp.float32) * sc, 'w2': jax.random.normal(ks[5], (E, H, I), dtype=jnp.float32) * sc, 'b2': jax.random.normal(ks[6], (E, H), dtype=jnp.float32) * sc}
    _L0_ffn_all = _L0_ffn_setup()
    _L0_ffn_in = {k: v for k, v in _L0_ffn_all.items() if k in ('gate_w', 'gate_b', 'w1', 'b1', 'w2', 'b2')}
    del _L0_ffn_all
    return {'x': x, 'ctx_1024': ctx_1024, 'g_xattn': g_xattn, 'g_ffn': g_ffn, 'L0_xattn_in_proj_w': _L0_xattn_in['in_proj_w'], 'L0_xattn_conv_w': _L0_xattn_in['conv_w'], 'L0_xattn_conv_b': _L0_xattn_in['conv_b'], 'L0_xattn_x_proj_w': _L0_xattn_in['x_proj_w'], 'L0_xattn_dt_proj_w': _L0_xattn_in['dt_proj_w'], 'L0_xattn_dt_proj_b': _L0_xattn_in['dt_proj_b'], 'L0_xattn_A_log': _L0_xattn_in['A_log'], 'L0_xattn_D': _L0_xattn_in['D'], 'L0_ffn_gate_w': _L0_ffn_in['gate_w'], 'L0_ffn_gate_b': _L0_ffn_in['gate_b'], 'L0_ffn_w1': _L0_ffn_in['w1'], 'L0_ffn_b1': _L0_ffn_in['b1'], 'L0_ffn_w2': _L0_ffn_in['w2'], 'L0_ffn_b2': _L0_ffn_in['b2']}

def reference(x, ctx_1024, g_xattn, g_ffn, L0_xattn_in_proj_w, L0_xattn_conv_w, L0_xattn_conv_b, L0_xattn_x_proj_w, L0_xattn_dt_proj_w, L0_xattn_dt_proj_b, L0_xattn_A_log, L0_xattn_D, L0_ffn_gate_w, L0_ffn_gate_b, L0_ffn_w1, L0_ffn_b1, L0_ffn_w2, L0_ffn_b2):
    import jax
    import jax.numpy as jnp

    def _L0_xattn_ref(hidden_states, z, in_proj_w, conv_w, conv_b, x_proj_w, dt_proj_w, dt_proj_b, A_log, D):
        import jax, jax.numpy as jnp
        import numpy as np
        import math
        B, L, DM = (2, 512, 256)
        DS, DC, EXP = (16, 4, 2)
        DI = EXP * DM
        DR = math.ceil(DM / 16)
        DT_MIN, DT_MAX, DT_FLOOR = (0.001, 0.1, 0.0001)

        def _ssm_forward(hidden_states, z, in_proj_w, conv_w, conv_b, x_proj_w, dt_proj_w, dt_proj_b, A_log, D):
            b = hidden_states.shape[0]
            x = jnp.einsum('ed,bld->bel', in_proj_w, hidden_states)
            xp = jnp.pad(x, ((0, 0), (0, 0), (DC - 1, 0)))
            xc = jax.lax.conv_general_dilated(xp, conv_w[:, None, :], window_strides=(1,), padding='VALID', dimension_numbers=('NCH', 'OIH', 'NCH'), feature_group_count=DI)
            u = jax.nn.silu(xc + conv_b[None, :, None])
            x_dbl = jnp.einsum('ke,bel->bkl', x_proj_w, u)
            dt_lo = x_dbl[:, :DR]
            Bm = x_dbl[:, DR:DR + DS]
            Cm = x_dbl[:, DR + DS:]
            delta = jax.nn.softplus(jnp.einsum('er,brl->bel', dt_proj_w, dt_lo) + dt_proj_b[None, :, None])
            A = -jnp.exp(A_log)

            def step(state, xs):
                d_t, B_t, C_t, u_t = xs
                dA = jnp.exp(d_t[..., None] * A)
                state = state * dA + (d_t * u_t)[..., None] * B_t[:, None, :]
                y_t = jnp.einsum('ben,bn->be', state, C_t)
                return (state, y_t)
            xs = (jnp.moveaxis(delta, -1, 0), jnp.moveaxis(Bm, -1, 0), jnp.moveaxis(Cm, -1, 0), jnp.moveaxis(u, -1, 0))
            state0 = jnp.zeros((b, DI, DS), delta.dtype)
            _, ys = jax.lax.scan(step, state0, xs)
            y = jnp.moveaxis(ys, 0, -1)
            y = y + D[None, :, None] * u
            y = y * jax.nn.silu(z)
            return jnp.swapaxes(y, 1, 2)
        return _ssm_forward(hidden_states, z, in_proj_w, conv_w, conv_b, x_proj_w, dt_proj_w, dt_proj_b, A_log, D)

    def _L0_ffn_ref(hidden_states, gate_w, gate_b, w1, b1, w2, b2):
        import jax, jax.numpy as jnp
        import numpy as np
        NUM_EXPERTS = 8
        TOP_K = 2
        B, S, H = hidden_states.shape
        x = hidden_states.reshape(-1, H)
        logits = x @ gate_w.T + gate_b
        top_vals, top_idx = jax.lax.top_k(logits, TOP_K)
        routing = jax.nn.softmax(top_vals.astype(jnp.float32), axis=-1).astype(x.dtype)
        out = jnp.zeros_like(x)
        E = w1.shape[0]
        for e in range(E):
            h = x @ w1[e].T + b1[e]
            x_glu = h[:, 0::2]
            x_lin = h[:, 1::2]
            y = x_glu * jax.nn.sigmoid(1.702 * x_glu) * (x_lin + 1.0)
            ye = y @ w2[e].T + b2[e]
            we = jnp.sum(routing * (top_idx == e), axis=-1)
            out = out + ye * we[:, None]
        return out.reshape(B, S, H)
    x = x + jnp.tanh(g_xattn[0]) * _L0_xattn_ref(ctx_1024, _layernorm(x, axis=-1), L0_xattn_in_proj_w, L0_xattn_conv_w, L0_xattn_conv_b, L0_xattn_x_proj_w, L0_xattn_dt_proj_w, L0_xattn_dt_proj_b, L0_xattn_A_log, L0_xattn_D)
    x = x + jnp.tanh(g_ffn[0]) * _L0_ffn_ref(_layernorm(x, axis=-1), L0_ffn_gate_w, L0_ffn_gate_b, L0_ffn_w1, L0_ffn_b1, L0_ffn_w2, L0_ffn_b2)
    return x

_drawn_inputs = setup_inputs


def setup_inputs(seed=0):
    import zlib

    import numpy as np

    out = dict(_drawn_inputs(seed))
    spreads = {'L0_xattn_conv_b': (0.0, 0.1), 'L0_xattn_D': (1.0, 0.2)}
    factors = {'L0_xattn_dt_proj_w': 5.507, 'L0_ffn_gate_b': 4.043, 'L0_ffn_b1': 8.0, 'L0_ffn_b2': 4.362}
    for name, (base, spread) in spreads.items():
        noise = np.random.default_rng([zlib.crc32(name.encode()), seed]).standard_normal(out[name].shape)
        drawn = base * np.exp(spread * noise) if base else spread * noise
        out[name] = jnp.asarray(drawn.astype(out[name].dtype))
    for name, factor in factors.items():
        out[name] = (out[name] * factor).astype(out[name].dtype)
    return out
```

```python
from contextlib import ExitStack

import numpy as np

import concourse.bass as bass
from concourse import mybir

F32 = mybir.dt.float32
F32R = mybir.dt.float32r
I32 = mybir.dt.int32
U32 = mybir.dt.uint32
AX = mybir.AxisListType
ALU = mybir.AluOpType
ACT = mybir.ActivationFunctionType

P = 128
B, L, DM = 4, 512, 256
DI, DS, DR, DC = 512, 16, 16, 4
ET = DI // P
LT = L // P
KC = DM // P
HALF = DS // 2
UNITS = ET * DS
EPS = 1e-5
H, I, E, TOP = 512, 512, 8, 2
HC, IC = H // P, I // P
NT = B * LT
SLOTS = (TOP * NT * P + E * P - 1) // P
WCOLS = HC * 2 * I + IC * H
BCOLS = 2 * I + H
CONSTS = 4 * P + SLOTS + E
CW, CB, CD, CDT, CA = 0, DC, DC + 1, DC + 2, DC + 3
NCH = DC + 3 + DS

PRIME = 4


def unit(k):
    g = k // HALF
    return g, g % ET, g // ET, k % HALF


def mamba_block(nc, ctx, x2_all, x, ctxT, inT, chan, xprojT, dtT, ident_d, g_x, bc_dram, xs_dram):

    def sb(name, shape, dt=F32):
        return ctx.enter_context(nc.sbuf_tensor(name, shape, dt))

    def sem(name):
        return ctx.enter_context(nc.semaphore(name))

    ctx_sb = sb("ctx_sb", [P, KC, L])
    inT_sb = sb("inT_sb", [P, KC, DI])
    chan_sb = sb("chan_sb", [P, ET, NCH])
    a_neg = sb("a_neg", [P, ET, DS])
    xprojT_sb = sb("xprojT_sb", [P, ET, DR + 2 * DS])
    dtT_sb = sb("dtT_sb", [DR, DI])
    ident = sb("ident_sb", [P, P])
    diag_d = sb("diag_d", [P, ET, P])
    gate = sb("gate", [P, 1])
    half_pow = sb("half_pow", [P, ET])
    stats = sb("stats", [P, ET, 6])
    mean_var = sb("mean_var", [P, ET, 2])
    rstd = sb("rstd", [P, ET])
    neg_mr = sb("neg_mr", [P, ET])
    u = sb("u", [P, 2, ET, L])
    delta = sb("delta", [P, 2, ET, L])
    du = sb("du", [P, 2, ET, L])
    sz = sb("sz", [P, 2, ET, L])
    xd = sb("xd", [DR + 2 * DS, L])
    bc = sb("bc", [P, 2, 2, HALF, L])
    dbu = sb("dbu", [P, 2, 2, L])
    hc = sb("hc", [P, 4, L])
    y_half = sb("y_half", [P, ET, L])
    yz = sb("yz", [P, 2, L])
    zeros = sb("zeros", [P, H])

    decay = ctx.enter_context(nc.psum_tensor("decay", [P, 4, L], F32))
    y_ps = ctx.enter_context(nc.psum_tensor("y_ps", [P, 2, L], F32))
    proj = ctx.enter_context(nc.psum_tensor("proj", [P, L], F32))
    turned = ctx.enter_context(nc.psum_tensor("turned", [P, LT, P], F32))

    consts_in = sem("consts_in")
    consts_made = sem("consts_made")
    signs_made = sem("signs_made")
    pows_made = sem("pows_made")
    a_exp = sem("a_exp")
    x_in = sem("x_in")
    ctx_in = sem("ctx_in")
    xs_out = sem("xs_out")
    bc_in = [sem("bc_in0"), sem("bc_in1")]
    stats_done = sem("stats_done")
    aggr_done = sem("aggr_done")
    var_eps = sem("var_eps")
    rstd_done = sem("rstd_done")
    ln_done = sem("ln_done")
    inproj_done = sem("inproj_done")
    tap_done = sem("tap_done")
    conv_step = sem("conv_step")
    conv_done = sem("conv_done")
    u_done = sem("u_done")
    sz_done = sem("sz_done")
    xd_mm = sem("xd_mm")
    xd_done = sem("xd_done")
    delta_mm = sem("delta_mm")
    sp_read = sem("sp_read")
    sp_exp = sem("sp_exp")
    sp_ln = sem("sp_ln")
    delta_done = sem("delta_done")
    du_done = sem("du_done")
    decay_done = sem("decay_done")
    dbu_done = sem("dbu_done")
    scan_done = sem("scan_done")
    hc_done = sem("hc_done")
    acc_done = sem("acc_done")
    half_saved = sem("half_saved")
    gated = sem("gated")
    turned_done = sem("turned_done")
    x2_done = sem("x2_done")
    zeros_made = sem("zeros_made")
    slots_cleared = sem("slots_cleared")

    def at(i, n=1):
        return bass.ds(i, n)

    block = ctx.enter_context(nc.Block())

    @block.sync
    def _(sp):
        sp.dma_start(inT_sb[:], inT).then_inc(consts_in, 16)
        sp.dma_start(chan_sb[:], chan).then_inc(consts_in, 16)
        sp.dma_start(ident[:], ident_d).then_inc(consts_in, 16)

        def load_inputs(b):
            sp.wait_ge(inproj_done, ET * b + PRIME)
            sp.dma_start(ctx_sb[:], ctxT[at(b), :, :, :].rearrange("o k p l -> p (o k) l")).then_inc(ctx_in, 16)
            sp.dma_start(x2_all[:, at(b * LT, LT), :], x[at(b), :, :].rearrange("o (t p) d -> p (o t) d", p=P))\
              .then_inc(x_in, 16)

        def spread_bc(b, first=False):
            sp.wait_ge(xd_done, b + 1)
            sp.dma_start(bc_dram[at(b), :, :], xd[DR:, :]).then_inc(xs_out, 16)
            sp.wait_ge(xs_out, (b + 1) * 16)
            for h in range(2):
                if not first:
                    sp.wait_ge(hc_done, b * UNITS + PRIME - (UNITS // 2) * (1 - h))
                for s in range(2):
                    rows = bc_dram[at(b), s * DS + h * HALF:s * DS + (h + 1) * HALF, :]
                    sp.dma_start(bc[:, h, s, :, :].rearrange("p n l -> p (n l)"),
                                 rows.rearrange("o n l -> o (n l)").to_broadcast([P, HALF * L])).then_inc(bc_in[h], 16)

        load_inputs(0)
        sp.dma_start(xprojT_sb[:], xprojT).then_inc(consts_in, 16)
        sp.dma_start(dtT_sb[:], dtT).then_inc(consts_in, 16)
        sp.dma_start(gate[:], g_x.to_broadcast([P, 1])).then_inc(consts_in, 16)
        spread_bc(0, first=True)
        sp.wait_ge(zeros_made, 1)
        sp.dma_start(xs_dram.rearrange("(s p) d -> p s d", p=P), zeros[:].unsqueeze(1).to_broadcast([P, SLOTS, H]))\
          .then_inc(slots_cleared, 16)
        with sp.Fori(1, B) as b:
            sp.wait_ge(x_in, b * 16)
            load_inputs(b)
            spread_bc(b)
        sp.wait_ge(slots_cleared, 16)
        sp.wait_ge(x2_done, B * ET + 1)

    @block.tensor
    def _(pe):
        pe.sem_inc(acc_done, PRIME)
        pe.sem_inc(inproj_done, PRIME)
        pe.wait_ge(consts_in, 16 * 6)
        pe.wait_ge(consts_made, 1)

        def input_projection(b, t):
            pe.wait_ge(ctx_in, (b + 1) * 16)
            if t:
                pe.wait_ge(conv_done, b * ET + t)
            for c in range(KC):
                mm = pe.matmul(proj[:], inT_sb[:, c, t * P:(t + 1) * P], ctx_sb[:, c, :],
                               start=c == 0, stop=c == KC - 1)
            mm.then_inc(inproj_done, 1)

        def x_projection(b, p):
            pe.wait_ge(conv_done, b * ET + ET)
            pe.wait_ge(u_done, b * ET + ET)
            for t in range(ET):
                mm = pe.matmul(proj[0:DR + 2 * DS, :], xprojT_sb[:, t, :], u[:, at(p), t, :],
                               start=t == 0, stop=t == ET - 1)
            mm.then_inc(xd_mm, 1)

        def delta_projection(b, t):
            pe.wait_ge(xd_done, b + 1)
            if t:
                pe.wait_ge(sp_read, b * ET + t)
            pe.matmul(proj[:], dtT_sb[:, t * P:(t + 1) * P], xd[0:DR, :], start=True, stop=True)\
              .then_inc(delta_mm, 1)

        def turn(b, t):
            pe.wait_ge(gated, b * ET + t + 1 + PRIME)
            pe.wait_ge(x2_done, b * ET + t + 1)
            for l in range(LT):
                mm = pe.transpose(turned[:, l, :], yz[:, t % 2, l * P:(l + 1) * P], ident[:])
            mm.then_inc(turned_done, 1)

        def main(b, p, nb, np_):
            for k in range(UNITS):
                g, t, h, n = unit(k)
                if n == 0:
                    if g < 2:
                        pe.wait_ge(gated, b * ET + g + PRIME - 1)
                    elif g < ET + 2:
                        pe.wait_ge(half_saved, b * ET + g - 1)
                    else:
                        pe.wait_ge(gated, b * ET + g - ET - 1 + PRIME)
                    if h:
                        pe.wait_ge(half_saved, b * ET + t + 1)
                        pe.matmul(y_ps[:, g % 2, :], ident[:], y_half[:, t, :], start=True, stop=False)
                        pe.matmul(y_ps[:, g % 2, :], diag_d[:, t, :], u[:, at(p), t, :], start=False, stop=False)
                pe.wait_ge(hc_done, b * UNITS + k + 1 + PRIME)
                pe.matmul(y_ps[:, g % 2, :], ident[:], hc[:, k % 4, :], start=h == 0 and n == 0,
                          stop=n == HALF - 1).then_inc(acc_done, 1)
                if g > ET and n == 4:
                    turn(b, t - 1)
                if nb is not None:
                    if k in (2, 7, 12, 17):
                        input_projection(nb, (k - 2) // 5)
                    if k == 28:
                        x_projection(nb, np_)
                    if k in (34, 37, 40, 43):
                        delta_projection(nb, (k - 34) // 3)
            turn(b, ET - 1)

        for t in range(ET):
            input_projection(0, t)
        x_projection(0, 0)
        for t in range(ET):
            delta_projection(0, t)
        with pe.Fori(0, B - 1) as b:
            main(b, b % 2, b + 1, (b + 1) % 2)
        main(B - 1, (B - 1) % 2, None, None)

    @block.scalar
    def _(act):
        act.wait_ge(consts_in, 16 * 6)
        act.activation(gate[:], gate[:], ACT.Tanh).then_inc(a_exp, 1)
        act.activation(a_neg[:], chan_sb[:, :, CA:CA + DS], ACT.Exp).then_inc(a_exp, 1)

        def first_tap(b, p, t):
            act.wait_ge(inproj_done, b * ET + t + 1 + PRIME)
            act.activation(delta[:, at(p), t, :], proj[:], ACT.Identity, scale=chan_sb[:, t, CW + DC - 1:CW + DC],
                           bias=chan_sb[:, t, CB:CB + 1]).then_inc(tap_done, 1)

        def silus(b, p):
            for t in range(ET):
                act.wait_ge(conv_done, b * ET + t + 1)
                act.activation(u[:, at(p), t, :], delta[:, at(p), t, :], ACT.Silu).then_inc(u_done, 1)
            act.wait_ge(ln_done, b + 1)
            for t in range(ET):
                act.activation(sz[:, at(p), t, :], x2_all[:, at(b * LT + t), :], ACT.Silu,
                               scale=rstd[:, t:t + 1], bias=neg_mr[:, t:t + 1]).then_inc(sz_done, 1)

        def keep_xd(b, first=False):
            act.wait_ge(xd_mm, b + 1)
            if not first:
                act.wait_ge(xs_out, b * 16)
            act.activation(xd[:], proj[0:DR + 2 * DS, :], ACT.Copy).then_inc(xd_done, 1)

        def softplus(b, p, t):
            act.wait_ge(delta_mm, b * ET + t + 1)
            act.activation(du[:, at(p), t, :], proj[:], ACT.Relu, bias=chan_sb[:, t, CDT:CDT + 1])
            act.activation(delta[:, at(p), t, :], proj[:], ACT.Abs, bias=chan_sb[:, t, CDT:CDT + 1])\
               .then_inc(sp_read, 1)

        def softplus_exp(b, p, t):
            act.wait_ge(sp_read, sp_step)
            act.reg_add(sp_step, sp_step, 1)
            act.activation(delta[:, at(p), t, :], delta[:, at(p), t, :], ACT.Exp, scale=-1.0).then_inc(sp_exp, 1)

        def softplus_ln(b, p, t):
            act.wait_ge(sp_exp, ln_step)
            act.reg_add(ln_step, ln_step, 1)
            act.activation(delta[:, at(p), t, :], delta[:, at(p), t, :], ACT.Ln, bias=1.0).then_inc(sp_ln, 1)

        def save_half(b, g):
            act.wait_ge(acc_done, b * UNITS + HALF * (g + 1) + PRIME)
            act.activation(y_half[:, g, :], y_ps[:, g % 2, :], ACT.Copy).then_inc(half_saved, 1)

        def main(b, p, nb, np_):
            for k in range(UNITS):
                g, t, h, n = unit(k)
                if h == 0 and n == 0:
                    act.wait_ge(delta_done, b * ET + t + 1)
                act.wait_ge(hc_done, bank_free)
                act.reg_add(bank_free, bank_free, 1)
                act.activation(decay[:, k % 4, :], delta[:, at(p), t, :], ACT.Exp,
                               scale=a_neg[:, t, h * HALF + n:h * HALF + n + 1]).then_inc(decay_done, 1)
                if 1 <= g <= ET and n == 5:
                    save_half(b, g - 1)
                if nb is not None:
                    if k in (6, 11, 16, 21):
                        first_tap(nb, np_, (k - 6) // 5)
                    if k == 27:
                        silus(nb, np_)
                    if k == 34:
                        keep_xd(nb)
                    if k in (39, 42, 45, 48):
                        softplus(nb, np_, (k - 39) // 3)
                    if k in (40, 43, 46, 49):
                        softplus_exp(nb, np_, (k - 40) // 3)
                    if k == 50:
                        for t in range(ET):
                            softplus_ln(nb, np_, t)

        for t in range(ET):
            first_tap(0, 0, t)
        silus(0, 0)
        keep_xd(0, first=True)
        sp_step = act.alloc_register("sp_step")
        ln_step = act.alloc_register("ln_step")
        act.reg_mov(sp_step, 1)
        act.reg_mov(ln_step, 1)
        for t in range(ET):
            softplus(0, 0, t)
            softplus_exp(0, 0, t)
        for t in range(ET):
            softplus_ln(0, 0, t)
        act.wait_ge(signs_made, 1)
        bank_free = act.alloc_register("bank_free")
        act.reg_mov(bank_free, PRIME - 3)
        with act.Fori(0, B - 1) as b:
            main(b, b % 2, b + 1, (b + 1) % 2)
        main(B - 1, (B - 1) % 2, None, None)

    @block.gpsimd
    def _(pool):
        pool.memset(half_pow[:], -0.5).then_inc(pows_made, 1)

        def inverse_root(b):
            pool.wait_ge(sz_done, b * ET + PRIME)
            pool.wait_ge(aggr_done, rows_ready)
            pool.reg_add(rows_ready, rows_ready, ET)
            pool.tensor_scalar(rstd[:], mean_var[:, :, 1], EPS, 1.0, ALU.add, ALU.mult).then_inc(var_eps, 1)
            pool.wait_ge(var_eps, b + 1)
            pool.tensor_tensor(rstd[:], rstd[:], half_pow[:], ALU.pow).then_inc(rstd_done, 1)

        def main(b, p, nb):
            for j in range(UNITS // 2):
                g, t, h, n = unit(2 * j)
                if h == 0 and n == 0:
                    pool.wait_ge(du_done, b * ET + t + 1)
                if t == 0 and n == 0:
                    pool.wait_ge(bc_in[h], b * 32 + 32)
                pool.wait_ge(scan_done, buffer_free)
                pool.reg_add(buffer_free, buffer_free, 2)
                pool.tensor_tensor(dbu[:, j % 2, :, :], du[:, at(p), t, :].to_broadcast([P, 2, L]),
                                   bc[:, h, 0, n:n + 2, :], ALU.mult).then_inc(dbu_done, 1)
                if nb is not None and j == 4:
                    inverse_root(nb)

        pool.memset(zeros[:], 0.0).then_inc(zeros_made, 1)
        pool.sem_inc(sz_done, PRIME)
        pool.wait_ge(pows_made, 1)
        rows_ready = pool.alloc_register("rows_ready")
        buffer_free = pool.alloc_register("buffer_free")
        pool.reg_mov(rows_ready, ET)
        pool.reg_mov(buffer_free, PRIME - 2)
        inverse_root(0)
        with pool.Fori(0, B - 1) as b:
            main(b, b % 2, b + 1)
        main(B - 1, (B - 1) % 2, None)

    @block.vector
    def _(dve):
        dve.sem_inc(scan_done, PRIME)
        dve.sem_inc(hc_done, PRIME)
        dve.sem_inc(gated, PRIME)
        dve.sem_inc(x2_done, 1)
        dve.wait_ge(consts_in, 16 * 6)
        for t in range(ET):
            mk = dve.tensor_scalar(diag_d[:, t, :], ident[:], chan_sb[:, t, CD:CD + 1], None, ALU.mult)
        mk.then_inc(consts_made, 1)
        dve.wait_ge(a_exp, 2)
        dve.tensor_scalar(a_neg[:], a_neg[:], -1.0, None, ALU.mult).then_inc(signs_made, 1)

        def row_stats(b, t):
            if t == 0:
                dve.wait_ge(x_in, (b + 1) * 16)
            dve.bn_stats(stats[:, t, :], x2_all[:, at(b * LT + t), :]).then_inc(stats_done, 1)

        def row_aggr(b):
            dve.wait_ge(stats_done, rows_seen)
            dve.reg_add(rows_seen, rows_seen, ET)
            for t in range(ET):
                dve.bn_aggr(mean_var[:, t, :], stats[:, t, :]).then_inc(aggr_done, 1)

        def row_shift(b):
            dve.wait_ge(rstd_done, b + 1)
            dve.scalar_tensor_tensor(out=neg_mr[:], in0=mean_var[:, :, 0], scalar=-1.0, in1=rstd[:],
                                     op0=ALU.mult, op1=ALU.mult).then_inc(ln_done, 1)

        def conv(b, p, t):
            dve.wait_ge(tap_done, b * ET + t + 1)
            for s in range(1, DC):
                if s > 1:
                    dve.wait_ge(conv_step, b * 2 * ET + 2 * t + s - 1)
                w = chan_sb[:, t, CW + DC - 1 - s:CW + DC - s]
                acc = delta[:, at(p), t, s:]
                dve.scalar_tensor_tensor(out=acc, in0=proj[:, 0:L - s], scalar=w, in1=acc,
                                         op0=ALU.mult, op1=ALU.add).then_inc(conv_step if s < DC - 1 else conv_done, 1)

        def delta_du(b, p, t):
            d, v = delta[:, at(p), t, :], du[:, at(p), t, :]
            dve.wait_ge(sp_ln, b * ET + t + 1)
            dve.tensor_tensor(d, d, v, ALU.add).then_inc(delta_done, 1)
            dve.wait_ge(delta_done, b * ET + t + 1)
            dve.tensor_tensor(v, d, u[:, at(p), t, :], ALU.mult).then_inc(du_done, 1)

        def times_c(b, k):
            g, t, h, n = unit(k)
            if t == 0 and n == 0:
                dve.wait_ge(bc_in[h], b * 32 + 32)
            dve.wait_ge(scan_done, b * UNITS + k + 1 + PRIME)
            dve.wait_ge(acc_done, b * UNITS + k - 3 + PRIME)
            dve.tensor_tensor(hc[:, k % 4, :], decay[:, k % 4, :], bc[:, h, 1, n, :], ALU.mult).then_inc(hc_done, 1)

        def gate_y(b, p, t):
            g = ET + t
            dve.wait_ge(acc_done, b * UNITS + HALF * (g + 1) + PRIME)
            dve.tensor_tensor(yz[:, t % 2, :], y_ps[:, g % 2, :], sz[:, at(p), t, :], ALU.mult).then_inc(gated, 1)

        def residual(b, t):
            dve.wait_ge(turned_done, b * ET + t + 1)
            cols = x2_all[:, at(b * LT, LT), t * P:(t + 1) * P]
            dve.scalar_tensor_tensor(out=cols, in0=turned[:], scalar=gate[:, 0:1], in1=cols,
                                     op0=ALU.mult, op1=ALU.add).then_inc(x2_done, 1)

        def main(b, p, nb, np_):
            for k in range(UNITS):
                g, t, h, n = unit(k)
                dve.wait_ge(decay_done, b * UNITS + k + 1)
                if n % 2 == 0:
                    dve.wait_ge(dbu_done, b * (UNITS // 2) + k // 2 + 1)
                dve.tensor_tensor_scan(decay[:, k % 4, :], decay[:, k % 4, :], dbu[:, k // 2 % 2, k % 2, :], 0.0,
                                       ALU.mult, ALU.add).then_inc(scan_done, 1)
                if k:
                    times_c(b, k - 1)
                if g > ET and n == 2:
                    gate_y(b, p, t - 1)
                if g > ET and n == 6:
                    residual(b, t - 1)
                if nb is not None:
                    if k < ET:
                        row_stats(nb, k)
                    if k == 6:
                        row_aggr(nb)
                    if k == 12:
                        row_shift(nb)
                    if k in (5, 10, 15, 20):
                        conv(nb, np_, (k - 5) // 5)
                    if k in (50, 53, 56, 59):
                        delta_du(nb, np_, (k - 50) // 3)
            times_c(b, UNITS - 1)
            gate_y(b, p, ET - 1)
            residual(b, ET - 1)

        rows_seen = dve.alloc_register("rows_seen")
        dve.reg_mov(rows_seen, ET)
        for t in range(ET):
            row_stats(0, t)
        row_aggr(0)
        row_shift(0)
        for t in range(ET):
            conv(0, 0, t)
        for t in range(ET):
            delta_du(0, 0, t)
        with dve.Fori(0, B - 1) as b:
            main(b, b % 2, b + 1, (b + 1) % 2)
        main(B - 1, (B - 1) % 2, None, None)


def moe_block(nc, ctx, x2_all, out, w_all, b_all, gate_wT, gate_b, consts, g_ffn, xs_dram, ys_dram):

    def sb(name, shape, dt=F32):
        return ctx.enter_context(nc.sbuf_tensor(name, shape, dt))

    def sem(name):
        return ctx.enter_context(nc.semaphore(name))

    def at(i, n=1):
        return bass.ds(i, n)

    cst = sb("cst", [P, CONSTS])
    ident, before, ones = cst[:, 0:P], cst[:, P:2 * P], cst[:, 2 * P:3 * P]
    same_expert, slot_no, preference = (cst[:, 3 * P:4 * P], cst[:, 4 * P:4 * P + SLOTS],
                                        cst[:, 4 * P + SLOTS:4 * P + SLOTS + E])
    gwT = sb("gwT", [P, HC, E])
    gb = sb("gb", [P, E])
    gate2 = sb("gate2", [P, 1])
    neg_half = sb("neg_half", [P, NT])
    st2 = sb("st2", [P, NT, 6])
    mv2 = sb("mv2", [P, NT, 2])
    rs2 = sb("rs2", [P, NT])
    nmr2 = sb("nmr2", [P, NT])
    logits = sb("logits", [P, NT, E])
    rest = sb("rest", [P, NT, E])
    first = sb("first", [P, NT, E])
    second = sb("second", [P, NT, E])
    tmp = sb("tmp", [P, NT, E])
    chosen = sb("chosen", [P, E, NT])
    top = sb("top", [P, 2, NT])
    pick = sb("pick", [P, NT])
    prob = sb("prob", [P, 2, NT])
    count = sb("count", [P, E, NT])
    rank = sb("rank", [P, E, NT])
    blocks_f = sb("blocks_f", [P, E])
    blocks_i = sb("blocks_i", [P, E], I32)
    ends_f = sb("ends_f", [P, E])
    ends_i = sb("ends_i", [P, E], I32)
    base = sb("base", [P, E])
    past = sb("past", [P, SLOTS, E])
    slot_f = sb("slot_f", [P, SLOTS])
    slot_expert = sb("slot_expert", [P, SLOTS], I32)
    pos_f = sb("pos_f", [P, 2, NT])
    pos = sb("pos", [P, 2, NT], U32)

    rows = sb("rows", [P, 4, H])
    inner = sb("inner", [P, 4, I])
    rowsT = inner[:].rearrange("p q (c t) -> p q c t", c=HC)
    glu, sig, lin, act_y = (inner[:, q, :] for q in range(4))

    stage = sb("stage", [P, WCOLS])
    w_hi = sb("w_hi", [P, 2, WCOLS], F32R)
    w_lo = sb("w_lo", [P, 2, WCOLS], F32R)
    bias = sb("bias", [P, 2, BCOLS])
    xg = sb("xg", [P, H])
    xT_hi = sb("xT_hi", [P, HC, P], F32R)
    xT_lo = sb("xT_lo", [P, HC, P], F32R)
    yT_hi = sb("yT_hi", [P, IC, P], F32R)
    yT_lo = sb("yT_lo", [P, IC, P], F32R)
    yo = sb("yo", [P, H])

    banks = ctx.enter_context(nc.psum_tensor("banks", [P, 4, 512], F32))
    xT_ps, yT_ps, glu_ps, lin_ps = (banks[:, q, :] for q in range(4))
    out_ps = ctx.enter_context(nc.psum_tensor("out_ps", [P, H], F32))
    lg_ps = ctx.enter_context(nc.psum_tensor("lg_ps", [P, NT, E], F32))
    rank_ps = ctx.enter_context(nc.psum_tensor("rank_ps", [P, E, NT], F32))
    count_ps = ctx.enter_context(nc.psum_tensor("count_ps", [P, E, NT], F32))

    cst_in = sem("cst_in")
    gate2_done = sem("gate2_done")
    powers = sem("powers")
    st2_done = sem("st2_done")
    mv2_done = sem("mv2_done")
    var2_eps = sem("var2_eps")
    rs2_done = sem("rs2_done")
    nmr2_done = sem("nmr2_done")
    rows_done = sem("rows_done")
    rows_turned = sem("rows_turned")
    rowsT_done = sem("rowsT_done")
    logits_mm = sem("logits_mm")
    route = sem("route")
    chosen_done = sem("chosen_done")
    diff_done = sem("diff_done")
    exp_done = sem("exp_done")
    ranks_mm = sem("ranks_mm")
    routed = sem("routed")
    rows_again = sem("rows_again")
    scattered = [sem(f"scattered{q}") for q in range(4)]
    w_in = sem("w_in")
    bias_in = sem("bias_in")
    hi_done = sem("hi_done")
    split_done = sem("split_done")
    xg_in = sem("xg_in")
    xT_mm = sem("xT_mm")
    xT_hi_done = sem("xT_hi_done")
    xT_lo_done = sem("xT_lo_done")
    glu_mm = sem("glu_mm")
    lin_mm = sem("lin_mm")
    glu_done = sem("glu_done")
    sig_done = sem("sig_done")
    lin_done = sem("lin_done")
    gs_done = sem("gs_done")
    act_done = sem("act_done")
    yT_mm = sem("yT_mm")
    yT_hi_done = sem("yT_hi_done")
    yT_lo_done = sem("yT_lo_done")
    out_mm = sem("out_mm")
    yo_done = sem("yo_done")
    ys_out = sem("ys_out")
    gathered = [sem(f"gathered{q}") for q in range(4)]
    combined = sem("combined")
    out_out = sem("out_out")

    block = ctx.enter_context(nc.Block())

    @block.sync
    def _(sp):
        sp.dma_start(cst[:], consts).then_inc(cst_in, 16)
        sp.dma_start(gwT[:], gate_wT).then_inc(cst_in, 16)
        sp.dma_start(gb[:], gate_b.to_broadcast([P, E])).then_inc(cst_in, 16)
        sp.dma_start(gate2[:], g_ffn.to_broadcast([P, 1])).then_inc(cst_in, 16)
        sp.sem_inc(ys_out, 16)
        for q in range(4):
            sp.wait_ge(scattered[q], 16 * 2 * NT // 4)
        def load_slot(s):
            sp.wait_ge(xT_mm, s)
            sp.dma_start(xg[:], xs_dram[at(s * P, P), :]).then_inc(xg_in, 16)

        def store_slot(s):
            sp.wait_ge(yo_done, s + 1 + PRIME)
            sp.dma_start(ys_dram[at(s * P, P), :], yo[:]).then_inc(ys_out, 16)

        sp.dma_start(xg[:], xs_dram[0:P, :]).then_inc(xg_in, 16)
        load_slot(1)
        with sp.Fori(1, SLOTS - 1) as s:
            load_slot(s + 1)
            store_slot(s - 1)
        store_slot(SLOTS - 2)
        store_slot(SLOTS - 1)
        with sp.Fori(0, NT) as i:
            sp.wait_ge(combined, 2 * i + 2)
            sp.dma_start(out[at(i * P, P), :], x2_all[:, at(i), :].rearrange("p o d -> p (o d)")).then_inc(out_out, 16)
        sp.wait_ge(out_out, 16 * NT)

    @block.tensor
    def _(pe):
        pe.sem_inc(logits_mm, PRIME)
        pe.sem_inc(rows_turned, PRIME)
        pe.wait_ge(cst_in, 64)
        with pe.Fori(0, NT // 4) as j:
            for q in range(4):
                pe.wait_ge(rows_done, j * 4 + q + 1)
                pe.wait_ge(rowsT_done, j * 4 + q - 3 + PRIME)
                for c in range(HC):
                    mm = pe.transpose(banks[:, q, c * P:(c + 1) * P], rows[:, q, c * P:(c + 1) * P], ident)
                mm.then_inc(rows_turned, 1)
            for q in range(4):
                pe.wait_ge(rowsT_done, j * 4 + q + 1 + PRIME)
                for c in range(HC):
                    mm = pe.matmul(lg_ps[:, at(j * 4 + q), :], rowsT[:, q, c, :], gwT[:, c, :],
                                   start=c == 0, stop=c == HC - 1)
                mm.then_inc(logits_mm, 1)
        pe.wait_ge(chosen_done, 1)
        pe.matmul(rank_ps[:], before, chosen[:], start=True, stop=True)
        pe.matmul(count_ps[:], ones, chosen[:], start=True, stop=True).then_inc(ranks_mm, 1)

        def turn_x(s):
            pe.wait_ge(xg_in, s * 16 + 16)
            pe.wait_ge(xT_lo_done, s + PRIME)
            for c in range(HC):
                mm = pe.transpose(xT_ps[:, c * P:(c + 1) * P], xg[:, c * P:(c + 1) * P], ident)
            mm.then_inc(xT_mm, 1)

        def turn_y(s):
            pe.wait_ge(act_done, s + 1)
            pe.wait_ge(yT_lo_done, s + PRIME)
            for c in range(IC):
                mm = pe.transpose(yT_ps[:, c * P:(c + 1) * P], act_y[:, c * P:(c + 1) * P], ident)
            mm.then_inc(yT_mm, 1)

        def product(acc, hi, lo, chunks, par, col, width, done):
            for c in range(chunks):
                for n, (a, w) in enumerate(((hi, w_hi), (hi, w_lo), (lo, w_hi))):
                    cols = w[:, at(par), col + c * width:col + c * width + 512]
                    mm = pe.matmul(acc, a[:, c, :], cols.rearrange("p o n -> p (o n)"),
                                   start=c == 0 and n == 0, stop=c == chunks - 1 and n == 2)
            mm.then_inc(done, 1)

        def up(s, e, half):
            if half == 0:
                pe.wait_ge(split_done, e + 1)
                pe.wait_ge(xT_lo_done, s + 1 + PRIME)
                pe.wait_ge(glu_done, s + PRIME)
                product(glu_ps, xT_hi, xT_lo, HC, e % 2, 0, 2 * I, glu_mm)
            else:
                pe.wait_ge(lin_done, s + PRIME)
                product(lin_ps, xT_hi, xT_lo, HC, e % 2, I, 2 * I, lin_mm)

        def down(s, par):
            pe.wait_ge(yT_lo_done, s + 1 + PRIME)
            pe.wait_ge(yo_done, s + PRIME)
            product(out_ps[:], yT_hi, yT_lo, IC, par, HC * 2 * I, H, out_mm)

        turn_x(0)
        up(0, 0, 0)
        up(0, 0, 1)
        turn_x(1)
        with pe.Fori(1, SLOTS - 1) as s:
            e = pe.value_load(slot_expert[0:1, at(s)], min_val=0, max_val=E - 1)
            e_last = pe.value_load(slot_expert[0:1, at(s - 1)], min_val=0, max_val=E - 1)
            up(s, e, 0)
            turn_y(s - 1)
            up(s, e, 1)
            turn_x(s + 1)
            down(s - 1, e_last % 2)
        e = pe.value_load(slot_expert[0:1, SLOTS - 1:SLOTS], min_val=0, max_val=E - 1)
        e_last = pe.value_load(slot_expert[0:1, SLOTS - 2:SLOTS - 1], min_val=0, max_val=E - 1)
        up(SLOTS - 1, e, 0)
        turn_y(SLOTS - 2)
        up(SLOTS - 1, e, 1)
        down(SLOTS - 2, e_last % 2)
        turn_y(SLOTS - 1)
        down(SLOTS - 1, e % 2)

    @block.scalar
    def _(act):
        act.wait_ge(cst_in, 64)
        act.activation(gate2[:], gate2[:], ACT.Tanh).then_inc(gate2_done, 1)
        act.wait_ge(nmr2_done, 1)
        turned = act.alloc_register("turned")
        act.reg_mov(turned, PRIME - 3)
        with act.Fori(0, NT // 4) as j:
            for q in range(4):
                act.wait_ge(rows_turned, turned)
                act.reg_add(turned, turned, 1)
                act.activation(rows[:, q, :], x2_all[:, at(j * 4 + q), :], ACT.Identity,
                               scale=rs2[:, at(j * 4 + q)], bias=nmr2[:, at(j * 4 + q)]).then_inc(rows_done, 1)
        act.wait_ge(diff_done, 1)
        act.activation(prob[:, 1, :], prob[:, 1, :], ACT.Exp).then_inc(exp_done, 1)
        act.wait_ge(rows_turned, NT + PRIME)
        for i in range(NT):
            if i >= 4:
                act.wait_ge(scattered[i % 4], 32 * (i // 4))
            act.activation(rows[:, i % 4, :], x2_all[:, i, :], ACT.Identity,
                           scale=rs2[:, i:i + 1], bias=nmr2[:, i:i + 1]).then_inc(rows_again, 1)

        def keep_xT(s):
            act.wait_ge(xT_mm, s + 1)
            act.activation(xT_hi[:].rearrange("p c t -> p (c t)"), xT_ps, ACT.Copy).then_inc(xT_hi_done, 1)

        def sigmoid(s):
            act.wait_ge(glu_done, s + 1 + PRIME)
            act.activation(sig, glu, ACT.Sigmoid, scale=1.702).then_inc(sig_done, 1)

        def keep_yT(s):
            act.wait_ge(yT_mm, s + 1)
            act.activation(yT_hi[:].rearrange("p c t -> p (c t)"), yT_ps, ACT.Copy).then_inc(yT_hi_done, 1)

        keep_xT(0)
        sigmoid(0)
        keep_xT(1)
        with act.Fori(1, SLOTS - 1) as s:
            sigmoid(s)
            keep_yT(s - 1)
            keep_xT(s + 1)
        sigmoid(SLOTS - 1)
        keep_yT(SLOTS - 2)
        keep_yT(SLOTS - 1)

    @block.vector
    def _(dve):
        steps = [0]

        def step(ins):
            steps[0] += 1
            ins.then_inc(route, 1)
            dve.wait_ge(route, steps[0])

        dve.sem_inc(rowsT_done, PRIME)
        dve.sem_inc(xT_lo_done, PRIME)
        dve.sem_inc(yT_lo_done, PRIME)
        dve.sem_inc(glu_done, PRIME)
        dve.sem_inc(lin_done, PRIME)
        dve.sem_inc(yo_done, PRIME)
        for i in range(NT):
            dve.bn_stats(st2[:, i, :], x2_all[:, i, :]).then_inc(st2_done, 1)
        dve.wait_ge(st2_done, NT)
        for i in range(NT):
            dve.bn_aggr(mv2[:, i, :], st2[:, i, :]).then_inc(mv2_done, 1)
        dve.wait_ge(rs2_done, 1)
        dve.scalar_tensor_tensor(out=nmr2[:], in0=mv2[:, :, 0], scalar=-1.0, in1=rs2[:],
                                 op0=ALU.mult, op1=ALU.mult).then_inc(nmr2_done, 1)
        with dve.Fori(0, NT // 4) as j:
            for q in range(4):
                dve.wait_ge(logits_mm, j * 4 + q - 3 + PRIME)
                dve.wait_ge(rows_turned, j * 4 + q + 1 + PRIME)
                dve.tensor_copy(rowsT[:, q, :, :].rearrange("p c t -> p (c t)"), banks[:, q, :])\
                   .then_inc(rowsT_done, 1)
        dve.wait_ge(logits_mm, NT + PRIME)

        def per_row(a):
            return a.unsqueeze(2).to_broadcast([P, NT, E])

        def per_expert(a, n=NT):
            return a.unsqueeze(1).to_broadcast([P, n, E])

        def choose(scores, value, onehot):
            step(dve.tensor_reduce(value, scores, AX.X, ALU.max))
            step(dve.tensor_tensor(tmp[:], scores, per_row(value), ALU.is_equal))
            step(dve.tensor_tensor(tmp[:], tmp[:], per_expert(preference), ALU.mult))
            step(dve.tensor_reduce(pick[:], tmp[:], AX.X, ALU.max))
            step(dve.tensor_tensor(onehot, per_expert(preference), per_row(pick[:]), ALU.is_equal))

        step(dve.tensor_tensor(logits[:], lg_ps[:], per_expert(gb[:]), ALU.add))
        choose(logits[:], top[:, 0, :], first[:])
        step(dve.scalar_tensor_tensor(out=rest[:], in0=first[:], scalar=-3.0e38, in1=logits[:],
                                      op0=ALU.mult, op1=ALU.add))
        choose(rest[:], top[:, 1, :], second[:])
        dve.tensor_tensor(chosen[:].rearrange("p e i -> p i e"), first[:], second[:], ALU.add).then_inc(chosen_done, 1)
        dve.tensor_tensor(prob[:, 1, :], top[:, 1, :], top[:, 0, :], ALU.subtract).then_inc(diff_done, 1)
        dve.wait_ge(ranks_mm, 1)
        flat = "p e i -> p (e i)"
        step(dve.tensor_tensor_scan(count[:].rearrange(flat), same_expert, count_ps[:].rearrange(flat), 0.0,
                                    ALU.mult, ALU.add))
        step(dve.tensor_scalar(blocks_f[:], count[:, :, NT - 1], 1.0, float(P - 1), ALU.max, ALU.add))
        step(dve.tensor_copy(blocks_i[:], blocks_f[:]))
        step(dve.tensor_scalar(blocks_i[:], blocks_i[:], 7, None, ALU.arith_shift_right))
        step(dve.tensor_copy(blocks_f[:], blocks_i[:]))
        step(dve.tensor_tensor_scan(ends_f[:], ones[:, 0:E], blocks_f[:], 0.0, ALU.mult, ALU.add))
        dve.tensor_copy(ends_i[:], ends_f[:])
        step(dve.tensor_tensor(base[:], ends_f[:], blocks_f[:], ALU.subtract))
        step(dve.tensor_scalar(base[:], base[:], float(P), None, ALU.mult))
        step(dve.tensor_tensor(rank[:], count[:], count_ps[:], ALU.subtract))
        step(dve.tensor_tensor(rank[:], rank[:], rank_ps[:], ALU.add))
        step(dve.tensor_tensor(rank[:], rank[:], base[:].unsqueeze(2).to_broadcast([P, E, NT]), ALU.add))
        for r, onehot in enumerate((first, second)):
            step(dve.tensor_tensor(tmp[:], onehot[:], rank[:].rearrange("p e i -> p i e"), ALU.mult))
            step(dve.tensor_reduce(pos_f[:, r, :], tmp[:], AX.X, ALU.add))
        step(dve.tensor_copy(pos[:], pos_f[:]))
        step(dve.tensor_tensor(past[:], slot_no.unsqueeze(2).to_broadcast([P, SLOTS, E]),
                               per_expert(ends_f[:], SLOTS), ALU.is_ge))
        step(dve.tensor_reduce(slot_f[:], past[:], AX.X, ALU.add))
        step(dve.tensor_scalar(slot_f[:], slot_f[:], float(E - 1), None, ALU.min))
        dve.tensor_copy(slot_expert[:], slot_f[:]).then_inc(routed, 1)
        dve.wait_ge(exp_done, 1)
        step(dve.tensor_scalar(pick[:], prob[:, 1, :], 1.0, None, ALU.add))
        step(dve.reciprocal(prob[:, 0, :], pick[:]))
        dve.wait_ge(gate2_done, 1)
        step(dve.tensor_scalar(prob[:, 0, :], prob[:, 0, :], gate2[:, 0:1], None, ALU.mult))
        step(dve.tensor_tensor(prob[:, 1, :], prob[:, 1, :], prob[:, 0, :], ALU.mult))

        def rest_of_xT(s):
            dve.wait_ge(xT_hi_done, s + 1)
            dve.tensor_tensor(xT_lo[:].rearrange("p c t -> p (c t)"), xT_ps,
                              xT_hi[:].rearrange("p c t -> p (c t)").bitcast(F32), ALU.subtract).then_inc(xT_lo_done, 1)

        def glu_bias(s, par):
            dve.wait_ge(glu_mm, s + 1)
            dve.tensor_tensor(glu, glu_ps, bias[:, at(par), 0:I].rearrange("p o n -> p (o n)"), ALU.add)\
               .then_inc(glu_done, 1)

        def activate(s, par):
            dve.wait_ge(sig_done, s + 1)
            dve.tensor_tensor(sig, glu, sig, ALU.mult).then_inc(gs_done, 1)
            dve.wait_ge(lin_mm, s + 1)
            dve.scalar_tensor_tensor(out=lin, in0=lin_ps, scalar=1.0, op0=ALU.add, op1=ALU.add,
                                     in1=bias[:, at(par), I:2 * I].rearrange("p o n -> p (o n)"))\
               .then_inc(lin_done, 1)
            dve.wait_ge(gs_done, s + 1)
            dve.wait_ge(lin_done, s + 1 + PRIME)
            dve.tensor_tensor(act_y, sig, lin, ALU.mult).then_inc(act_done, 1)

        def rest_of_yT(s):
            dve.wait_ge(yT_hi_done, s + 1)
            dve.tensor_tensor(yT_lo[:].rearrange("p c t -> p (c t)"), yT_ps,
                              yT_hi[:].rearrange("p c t -> p (c t)").bitcast(F32), ALU.subtract).then_inc(yT_lo_done, 1)

        def keep_out(s, par):
            dve.wait_ge(out_mm, s + 1)
            dve.wait_ge(ys_out, s * 16 + 16)
            dve.tensor_tensor(yo[:], out_ps[:], bias[:, at(par), 2 * I:].rearrange("p o n -> p (o n)"), ALU.add)\
               .then_inc(yo_done, 1)

        dve.wait_ge(routed, 1)
        rest_of_xT(0)
        dve.wait_ge(bias_in, 16)
        glu_bias(0, 0)
        rest_of_xT(1)
        activate(0, 0)
        with dve.Fori(1, SLOTS - 1) as s:
            e = dve.value_load(slot_expert[0:1, at(s)], min_val=0, max_val=E - 1)
            e_last = dve.value_load(slot_expert[0:1, at(s - 1)], min_val=0, max_val=E - 1)
            dve.wait_ge(bias_in, e * 16 + 16)
            glu_bias(s, e % 2)
            rest_of_yT(s - 1)
            rest_of_xT(s + 1)
            activate(s, e % 2)
            keep_out(s - 1, e_last % 2)
        e = dve.value_load(slot_expert[0:1, SLOTS - 1:SLOTS], min_val=0, max_val=E - 1)
        e_last = dve.value_load(slot_expert[0:1, SLOTS - 2:SLOTS - 1], min_val=0, max_val=E - 1)
        glu_bias(SLOTS - 1, e % 2)
        rest_of_yT(SLOTS - 2)
        activate(SLOTS - 1, e % 2)
        keep_out(SLOTS - 2, e_last % 2)
        rest_of_yT(SLOTS - 1)
        keep_out(SLOTS - 1, e % 2)
        for n in range(2 * NT):
            i, r = n // 2, n % 2
            dve.wait_ge(gathered[n % 4], 16 * (n // 4 + 1))
            if r:
                dve.wait_ge(combined, n)
            dve.scalar_tensor_tensor(out=x2_all[:, i, :], in0=rows[:, n % 4, :], scalar=prob[:, r, i:i + 1],
                                     in1=x2_all[:, i, :], op0=ALU.mult, op1=ALU.add).then_inc(combined, 1)

    @block.gpsimd
    def _(pool):
        pool.memset(neg_half[:], -0.5).then_inc(powers, 1)

        def load_expert(e):
            pool.dma_start(stage[:], w_all[at(e), :, :].rearrange("o p n -> p (o n)")).then_inc(w_in, 16)

        def split_expert(e, par):
            pool.dma_start(bias[:, par, :], b_all[at(e), :].to_broadcast([P, BCOLS])).then_inc(bias_in, 16)
            pool.wait_ge(w_in, loaded)
            pool.reg_add(loaded, loaded, 16)
            pool.tensor_copy(w_hi[:, par, :], stage[:]).then_inc(hi_done, 1)
            pool.wait_ge(hi_done, e + 1)
            pool.tensor_tensor(w_lo[:, par, :], stage[:], w_hi[:, par, :].bitcast(F32), ALU.subtract)\
                .then_inc(split_done, 1)
            pool.wait_ge(bias_in, e * 16 + 16)

        pool.wait_ge(powers, 1)
        pool.wait_ge(mv2_done, NT)
        pool.tensor_scalar(rs2[:], mv2[:, :, 1], EPS, 1.0, ALU.add, ALU.mult).then_inc(var2_eps, 1)
        pool.wait_ge(var2_eps, 1)
        pool.tensor_tensor(rs2[:], rs2[:], neg_half[:], ALU.pow).then_inc(rs2_done, 1)
        loaded = pool.alloc_register("loaded")
        pool.reg_mov(loaded, 16)
        load_expert(0)
        split_expert(0, 0)
        pool.wait_ge(split_done, 1)
        load_expert(1)
        pool.wait_ge(routed, 1)
        for n in range(2 * NT):
            i, r = n // 2, n % 2
            pool.wait_ge(rows_again, i + 1)
            pool.indirect_dma_start(out=xs_dram, out_offset=bass.IndirectOffsetOnAxis(ap=pos[:, r, i:i + 1], axis=0),
                                    in_=rows[:, i % 4, :], in_offset=None).then_inc(scattered[i % 4], 16)
        split_expert(1, 1)
        with pool.Fori(1, E // 2) as j:
            for q in range(2):
                e = j * 2 + q
                pool.wait_ge(split_done, e)
                load_expert(e)
                end = pool.value_load(ends_i[0:1, at(e - 2)], min_val=1, max_val=SLOTS)
                pool.wait_ge(yo_done, end + PRIME)
                split_expert(e, q)
        pool.wait_ge(ys_out, 16 * SLOTS + 16)
        for n in range(2 * NT):
            i, r = n // 2, n % 2
            if n >= 4:
                pool.wait_ge(combined, n - 3)
            pool.indirect_dma_start(out=rows[:, n % 4, :], out_offset=None, in_=ys_dram,
                                    in_offset=bass.IndirectOffsetOnAxis(ap=pos[:, r, i:i + 1], axis=0))\
                .then_inc(gathered[n % 4], 16)



def build(nc, x, ctxT, inT, chan, xprojT, dtT, g_x, w_all, b_all, gate_wT, gate_b, g_ffn, consts, out):
    with ExitStack() as whole:
        x2_all = whole.enter_context(nc.sbuf_tensor("x2_all", [P, NT, H], F32))
        bc_dram = nc.dram_tensor("bc_dram", [B, 2 * DS, L], F32, kind="Internal").ap()
        xs_dram = nc.dram_tensor("xs_dram", [SLOTS * P, H], F32, kind="Internal").ap()
        ys_dram = nc.dram_tensor("ys_dram", [SLOTS * P, H], F32, kind="Internal").ap()
        with ExitStack() as ctx:
            mamba_block(nc, ctx, x2_all, x, ctxT, inT, chan, xprojT, dtT, consts[:, 0:P], g_x, bc_dram, xs_dram)
        with ExitStack() as ctx:
            moe_block(nc, ctx, x2_all, out.rearrange("b l d -> (b l) d"), w_all, b_all, gate_wT, gate_b, consts,
                      g_ffn, xs_dram, ys_dram)


def kernel(**inputs):
    from concourse import bacc
    from concourse.bass_utils import run_bass_kernel_spmd

    a = {k: np.asarray(v) for k, v in inputs.items()}

    def rows(w, chunks):
        return w.reshape(chunks, P, -1).transpose(1, 0, 2)

    chan = np.concatenate([rows(a["L0_xattn_" + n], ET) for n in ("conv_w", "conv_b", "D", "dt_proj_b", "A_log")], 2)
    w1 = a["L0_ffn_w1"].reshape(E, I, 2, H).transpose(0, 3, 2, 1).reshape(E, HC, P, 2 * I)
    w2 = a["L0_ffn_w2"].transpose(0, 2, 1).reshape(E, IC, P, H)
    w_all = np.concatenate([w.transpose(0, 2, 1, 3).reshape(E, P, -1) for w in (w1, w2)], 2)
    b1 = a["L0_ffn_b1"].reshape(E, I, 2).transpose(0, 2, 1).reshape(E, 2 * I)
    consts = np.concatenate([np.eye(P), np.triu(np.ones((P, P)), 1), np.ones((P, P)),
                             np.tile(np.arange(P) % NT > 0, (P, 1)), np.tile(np.arange(SLOTS), (P, 1)),
                             np.tile(E - np.arange(E), (P, 1))], 1).astype(np.float32)
    arrays = {
        "x": a["x"],
        "ctxT": a["ctx_1024"].transpose(0, 2, 1).reshape(B, KC, P, L),
        "inT": rows(a["L0_xattn_in_proj_w"].T, KC),
        "chan": chan,
        "xprojT": rows(a["L0_xattn_x_proj_w"].T, ET),
        "dtT": a["L0_xattn_dt_proj_w"].T,
        "g_x": a["g_xattn"].reshape(1, 1),
        "w_all": w_all,
        "b_all": np.concatenate([b1, a["L0_ffn_b2"]], 1),
        "gate_wT": rows(a["L0_ffn_gate_w"].T, HC),
        "gate_b": a["L0_ffn_gate_b"].reshape(1, E),
        "g_ffn": a["g_ffn"].reshape(1, 1),
        "consts": consts,
    }
    arrays = {k: np.ascontiguousarray(v) for k, v in arrays.items()}
    nc = bacc.Bacc("TRN2", target_bir_lowering=False, num_devices=1)
    args = [nc.dram_tensor(k, v.shape, F32, kind="ExternalInput").ap() for k, v in arrays.items()]
    out = nc.dram_tensor("out", (B, L, H), F32, kind="ExternalOutput").ap()
    build(nc, *args, out)
    got = run_bass_kernel_spmd(nc, [arrays], core_ids=[0])
    return got.results[0]["out"]
```

```python
from contextlib import ExitStack

import numpy as np

import concourse.bass as bass
from concourse import mybir

F32 = mybir.dt.float32
F32R = mybir.dt.float32r
I32 = mybir.dt.int32
U32 = mybir.dt.uint32
AX = mybir.AxisListType
ALU = mybir.AluOpType
ACT = mybir.ActivationFunctionType

P = 128
B, L, DM = 4, 512, 256
DI, DS, DR, DC = 512, 16, 16, 4
ET = DI // P
LT = L // P
KC = DM // P
HALF = DS // 2
UNITS = ET * DS
EPS = 1e-5
H, I, E, TOP = 512, 512, 8, 2
HC, IC = H // P, I // P
NT = B * LT
SLOTS = (TOP * NT * P + E * P - 1) // P
PAIRS = (SLOTS - 3) // 2
assert SLOTS == 2 * PAIRS + 3
WCOLS = HC * 2 * I + IC * H
BCOLS = 2 * I + H
CONSTS = 4 * P + SLOTS + E
CW, CB, CD, CDT, CA = 0, DC, DC + 1, DC + 2, DC + 3
NCH = DC + 3 + DS

PRIME = 8
RING = 8


IN_PROJ, TAP, CONV = (1, 7, 13, 19), (10, 16, 22, 28), (8, 14, 20, 26)
GATE_SILU, U_SILU = 26, 34
X_PROJ, KEEP_XD = (31, 32, 33, 34), 43
DELTA_PROJ, SOFTPLUS, SOFTPLUS_EXP, DELTA = (37, 39, 42, 45), (46, 48, 51, 54), 55, (56, 58, 60, 62)


def unit(k):
    g = k // HALF
    return g, g % ET, g // ET, k % HALF


def mamba_block(nc, ctx, x2_all, x, ctxT, inT, chan, xprojT, dtT, ident_d, g_x, bc_dram, xs_dram):

    def sb(name, shape, dt=F32):
        return ctx.enter_context(nc.sbuf_tensor(name, shape, dt))

    def sem(name):
        return ctx.enter_context(nc.semaphore(name))

    ctx_sb = sb("ctx_sb", [P, KC, L])
    inT_sb = sb("inT_sb", [P, KC, DI])
    chan_sb = sb("chan_sb", [P, ET, NCH])
    a_neg = sb("a_neg", [P, ET, DS])
    xprojT_sb = sb("xprojT_sb", [P, ET, DR + 2 * DS])
    dtT_sb = sb("dtT_sb", [DR, DI])
    ident = sb("ident_sb", [P, P])
    diag_d = sb("diag_d", [P, ET, P])
    gate = sb("gate", [P, 1])
    half_pow = sb("half_pow", [P, ET])
    stats = sb("stats", [P, ET, 6])
    mean_var = sb("mean_var", [P, ET, 2])
    rstd = sb("rstd", [P, ET])
    neg_mr = sb("neg_mr", [P, ET])
    u = sb("u", [P, ET, L])
    delta = sb("delta", [P, 2, ET, L])
    du = sb("du", [P, 2, ET, L])
    sz = sb("sz", [P, 2, ET, L])
    xd = sb("xd", [DR + 2 * DS, L])
    bc = sb("bc", [P, 2, 2, HALF, L])
    dbu = sb("dbu", [P, 2, 2, L])
    states = sb("states", [P, RING, L])
    yz = sb("yz", [P, 2, L])
    zeros = sb("zeros", [P, H])

    y_ps = ctx.enter_context(nc.psum_tensor("y_ps", [P, ET, L], F32))
    proj = ctx.enter_context(nc.psum_tensor("proj", [P, 2, L], F32))
    turned = ctx.enter_context(nc.psum_tensor("turned", [P, LT, P], F32))

    consts_in = sem("consts_in")
    consts_made = sem("consts_made")
    signs_made = sem("signs_made")
    pows_made = sem("pows_made")
    a_exp = sem("a_exp")
    x_in = sem("x_in")
    ctx_in = sem("ctx_in")
    xs_out = sem("xs_out")
    bc_in = [[sem(f"{name}_in{h}") for name in ("b", "c")] for h in range(2)]
    stats_done = sem("stats_done")
    aggr_done = sem("aggr_done")
    var_eps = sem("var_eps")
    rstd_done = sem("rstd_done")
    ln_done = sem("ln_done")
    inproj_done = sem("inproj_done")
    tap_done = sem("tap_done")
    conv_step = sem("conv_step")
    conv_done = sem("conv_done")
    u_done = sem("u_done")
    sz_done = sem("sz_done")
    xd_mm = sem("xd_mm")
    xd_done = sem("xd_done")
    delta_mm = sem("delta_mm")
    sp_read = sem("sp_read")
    sp_exp = sem("sp_exp")
    sp_ln = sem("sp_ln")
    delta_done = sem("delta_done")
    du_done = sem("du_done")
    decay_done = sem("decay_done")
    dbu_done = sem("dbu_done")
    scan_done = sem("scan_done")
    hc_done = sem("hc_done")
    acc_done = sem("acc_done")
    gated = sem("gated")
    turned_done = sem("turned_done")
    x2_done = sem("x2_done")
    zeros_made = sem("zeros_made")
    slots_cleared = sem("slots_cleared")

    def at(i, n=1):
        return bass.ds(i, n)

    block = ctx.enter_context(nc.Block())

    @block.sync
    def _(sp):
        sp.dma_start(inT_sb[:], inT).then_inc(consts_in, 16)
        sp.dma_start(chan_sb[:], chan).then_inc(consts_in, 16)
        sp.dma_start(ident[:], ident_d).then_inc(consts_in, 16)

        def load_inputs(b):
            sp.wait_ge(inproj_done, ET * b + PRIME)
            sp.dma_start(ctx_sb[:], ctxT[at(b), :, :, :].rearrange("o k p l -> p (o k) l")).then_inc(ctx_in, 16)
            sp.dma_start(x2_all[:, at(b * LT, LT), :], x[at(b), :, :].rearrange("o (t p) d -> p (o t) d", p=P))\
              .then_inc(x_in, 16)

        def store_bc(b):
            sp.wait_ge(xd_done, b + 1)
            sp.dma_start(bc_dram[at(b), :, :], xd[DR:, :]).then_inc(xs_out, 16)
            sp.wait_ge(xs_out, (b + 1) * 16)

        def spread_half(b, h, first=False):
            if not first:
                sp.wait_ge(hc_done, b * UNITS + PRIME - (UNITS // 2) * (1 - h))
            for s in range(2):
                rows = bc_dram[at(b), s * DS + h * HALF:s * DS + (h + 1) * HALF, :]
                sp.dma_start(bc[:, h, s, :, :].rearrange("p n l -> p (n l)"),
                             rows.rearrange("o n l -> o (n l)").to_broadcast([P, HALF * L])).then_inc(bc_in[h][s], 16)

        load_inputs(0)
        sp.dma_start(xprojT_sb[:], xprojT).then_inc(consts_in, 16)
        sp.dma_start(dtT_sb[:], dtT).then_inc(consts_in, 16)
        sp.dma_start(gate[:], g_x.to_broadcast([P, 1])).then_inc(consts_in, 16)
        store_bc(0)
        spread_half(0, 0, first=True)
        sp.wait_ge(x_in, 16)
        load_inputs(1)
        spread_half(0, 1, first=True)
        with sp.Fori(1, B - 1) as b:
            store_bc(b)
            spread_half(b, 0)
            sp.wait_ge(x_in, b * 16 + 16)
            load_inputs(b + 1)
            spread_half(b, 1)
        store_bc(B - 1)
        spread_half(B - 1, 0)
        spread_half(B - 1, 1)
        sp.wait_ge(zeros_made, 1)
        sp.dma_start(xs_dram.rearrange("(s p) d -> p s d", p=P), zeros[:].unsqueeze(1).to_broadcast([P, SLOTS, H]))\
          .then_inc(slots_cleared, 16)
        sp.wait_ge(slots_cleared, 16)
        sp.wait_ge(x2_done, B * ET + 1)

    @block.tensor
    def _(pe):
        pe.sem_inc(acc_done, PRIME)
        pe.sem_inc(inproj_done, PRIME)
        pe.wait_ge(consts_in, 16 * 6)
        pe.wait_ge(consts_made, 1)

        def input_projection(b, t, first=False):
            pe.wait_ge(ctx_in, (b + 1) * 16)
            if t > 1 and not first:
                pe.wait_ge(conv_done, b * ET + t - 1)
            for c in range(KC):
                mm = pe.matmul(y_ps[:, t, :] if first else proj[:, t % 2, :], inT_sb[:, c, t * P:(t + 1) * P],
                               ctx_sb[:, c, :], start=c == 0, stop=c == KC - 1)
            mm.then_inc(inproj_done, 1)

        def x_projection(b, t):
            if t == 0:
                pe.wait_ge(conv_done, b * ET + ET)
                pe.wait_ge(u_done, b + 1)
            mm = pe.matmul(proj[0:DR + 2 * DS, 0, :], xprojT_sb[:, t, :], u[:, t, :],
                           start=t == 0, stop=t == ET - 1)
            if t == ET - 1:
                mm.then_inc(xd_mm, 1)

        def delta_projection(b, t, first=False):
            pe.wait_ge(xd_done, b + 1)
            if t > 1 and not first:
                pe.wait_ge(sp_read, b * ET + t - 1)
            pe.matmul(y_ps[:, t, :] if first else proj[:, t % 2, :], dtT_sb[:, t * P:(t + 1) * P], xd[0:DR, :],
                      start=True, stop=True).then_inc(delta_mm, 1)

        def turn(b, t):
            pe.wait_ge(gated, b * ET + t + 1 + PRIME)
            pe.wait_ge(x2_done, b * ET + t + 1)
            for l in range(LT):
                mm = pe.transpose(turned[:, l, :], yz[:, t % 2, l * P:(l + 1) * P], ident[:])
            mm.then_inc(turned_done, 1)

        def main(b, nb):
            for k in range(UNITS):
                g, t, h, n = unit(k)
                if h == 0 and n == 0:
                    pe.wait_ge(gated, b * ET + t + 1 - ET + PRIME)
                    pe.matmul(y_ps[:, t, :], diag_d[:, t, :], u[:, t, :], start=True, stop=False)
                pe.wait_ge(hc_done, b * UNITS + k + 1 + PRIME)
                pe.matmul(y_ps[:, t, :], ident[:], states[:, k % RING, :], start=False,
                          stop=h == 1 and n == HALF - 1).then_inc(acc_done, 1)
                if g > ET and n == 4:
                    turn(b, t - 1)
                if nb is not None:
                    if k in IN_PROJ:
                        input_projection(nb, IN_PROJ.index(k))
                    if k in X_PROJ:
                        x_projection(nb, X_PROJ.index(k))
                    if k in DELTA_PROJ:
                        delta_projection(nb, DELTA_PROJ.index(k))
            turn(b, ET - 1)

        for t in range(ET):
            input_projection(0, t, first=True)
        for t in range(ET):
            x_projection(0, t)
        for t in range(ET):
            delta_projection(0, t, first=True)
        pe.wait_ge(sp_read, ET)
        with pe.Fori(0, B - 1) as b:
            main(b, b + 1)
        main(B - 1, None)

    @block.scalar
    def _(act):
        act.wait_ge(consts_in, 16 * 6)
        act.activation(gate[:], gate[:], ACT.Tanh).then_inc(a_exp, 1)
        act.activation(a_neg[:], chan_sb[:, :, CA:CA + DS], ACT.Exp).then_inc(a_exp, 1)

        def first_tap(b, p, t, first=False):
            act.wait_ge(inproj_done, b * ET + t + 1 + PRIME)
            act.activation(delta[:, at(p), t, :], y_ps[:, t, :] if first else proj[:, t % 2, :], ACT.Identity,
                           scale=chan_sb[:, t, CW + DC - 1:CW + DC], bias=chan_sb[:, t, CB:CB + 1]).then_inc(tap_done, 1)

        def silu_u(b, p, first=False):
            if not first:
                act.wait_ge(acc_done, u_summed)
                act.reg_add(u_summed, u_summed, UNITS)
                act.wait_ge(du_done, b * ET)
            act.wait_ge(conv_done, convolved)
            act.reg_add(convolved, convolved, ET)
            act.activation(u[:], delta[:, at(p), :, :], ACT.Silu).then_inc(u_done, 1)

        def silu_z(b, p):
            act.wait_ge(ln_done, b + 1)
            for t in range(ET):
                act.activation(sz[:, at(p), t, :], x2_all[:, at(b * LT + t), :], ACT.Silu,
                               scale=rstd[:, t:t + 1], bias=neg_mr[:, t:t + 1]).then_inc(sz_done, 1)

        def keep_xd(b, first=False):
            act.wait_ge(xd_mm, b + 1)
            if not first:
                act.wait_ge(xs_out, b * 16)
            act.activation(xd[:], proj[0:DR + 2 * DS, 0, :], ACT.Copy).then_inc(xd_done, 1)

        def softplus(b, p, t, first=False):
            v = y_ps[:, t, :] if first else proj[:, t % 2, :]
            act.wait_ge(delta_mm, b * ET + t + 1)
            act.activation(du[:, at(p), t, :], v, ACT.Relu, bias=chan_sb[:, t, CDT:CDT + 1])
            act.activation(delta[:, at(p), t, :], v, ACT.Abs, bias=chan_sb[:, t, CDT:CDT + 1]).then_inc(sp_read, 1)

        def softplus_exp(b, p):
            act.wait_ge(sp_read, sp_step)
            act.reg_add(sp_step, sp_step, ET)
            act.activation(delta[:, at(p), :, :], delta[:, at(p), :, :], ACT.Exp, scale=-1.0).then_inc(sp_exp, 1)

        def softplus_ln(b, p):
            act.wait_ge(sp_exp, ln_step)
            act.reg_add(ln_step, ln_step, 1)
            act.activation(delta[:, at(p), :, :], delta[:, at(p), :, :], ACT.Ln, bias=1.0).then_inc(sp_ln, 1)

        def main(b, p, nb, np_):
            for k in range(UNITS):
                g, t, h, n = unit(k)
                if h == 0 and n == 0:
                    act.wait_ge(delta_done, b * ET + t + 1)
                act.wait_ge(acc_done, ring_free)
                act.reg_add(ring_free, ring_free, 1)
                act.activation(states[:, k % RING, :], delta[:, at(p), t, :], ACT.Exp,
                               scale=a_neg[:, t, h * HALF + n:h * HALF + n + 1]).then_inc(decay_done, 1)
                if nb is not None:
                    if k in TAP:
                        first_tap(nb, np_, TAP.index(k))
                    if k == GATE_SILU:
                        silu_z(nb, np_)
                    if k == U_SILU:
                        silu_u(nb, np_)
                    if k == KEEP_XD:
                        keep_xd(nb)
                    if k in SOFTPLUS:
                        softplus(nb, np_, SOFTPLUS.index(k))
                    if k == SOFTPLUS_EXP:
                        softplus_exp(nb, np_)
                        softplus_ln(nb, np_)

        convolved = act.alloc_register("convolved")
        act.reg_mov(convolved, ET)
        for t in range(ET):
            first_tap(0, 0, t, first=True)
        silu_u(0, 0, first=True)
        keep_xd(0, first=True)
        sp_step = act.alloc_register("sp_step")
        ln_step = act.alloc_register("ln_step")
        act.reg_mov(sp_step, ET)
        act.reg_mov(ln_step, 1)
        for t in range(ET):
            softplus(0, 0, t, first=True)
        softplus_exp(0, 0)
        softplus_ln(0, 0)
        silu_z(0, 0)
        act.wait_ge(signs_made, 1)
        ring_free = act.alloc_register("ring_free")
        u_summed = act.alloc_register("u_summed")
        act.reg_mov(ring_free, PRIME + 1 - RING)
        act.reg_mov(u_summed, PRIME + HALF * (ET - 1) + 1)
        with act.Fori(0, B - 1) as b:
            main(b, b % 2, b + 1, (b + 1) % 2)
        main(B - 1, (B - 1) % 2, None, None)

    @block.gpsimd
    def _(pool):
        pool.memset(half_pow[:], -0.5).then_inc(pows_made, 1)

        def inverse_root(b):
            pool.wait_ge(sz_done, b * ET + PRIME)
            pool.wait_ge(aggr_done, rows_ready)
            pool.reg_add(rows_ready, rows_ready, ET)
            pool.tensor_scalar(rstd[:], mean_var[:, :, 1], EPS, 1.0, ALU.add, ALU.mult).then_inc(var_eps, 1)
            pool.wait_ge(var_eps, b + 1)
            pool.tensor_tensor(rstd[:], rstd[:], half_pow[:], ALU.pow).then_inc(rstd_done, 1)

        def times_u(b, p, t):
            pool.wait_ge(delta_done, deltas)
            pool.reg_add(deltas, deltas, 1)
            pool.tensor_tensor(du[:, at(p), t, :], delta[:, at(p), t, :], u[:, t, :], ALU.mult).then_inc(du_done, 1)

        def main(b, p, nb, np_):
            for j in range(UNITS // 2):
                g, t, h, n = unit(2 * j)
                if h == 0 and n == 0:
                    pool.wait_ge(du_done, du_step)
                    pool.reg_add(du_step, du_step, 1)
                if t == 0 and n == 0:
                    pool.wait_ge(bc_in[h][0], b * 16 + 16)
                pool.wait_ge(scan_done, buffer_free)
                pool.reg_add(buffer_free, buffer_free, 2)
                pool.tensor_tensor(dbu[:, j % 2, :, :], du[:, at(p), t, :].to_broadcast([P, 2, L]),
                                   bc[:, h, 0, n:n + 2, :], ALU.mult).then_inc(dbu_done, 1)
                if g < ET - 1 and n == 2:
                    times_u(b, p, t + 1)
                if nb is not None and j == 4:
                    inverse_root(nb)
                if nb is not None and 2 * j == DELTA[0] + 4:
                    times_u(nb, np_, 0)

        pool.memset(zeros[:], 0.0).then_inc(zeros_made, 1)
        pool.sem_inc(sz_done, PRIME)
        pool.wait_ge(pows_made, 1)
        rows_ready = pool.alloc_register("rows_ready")
        buffer_free = pool.alloc_register("buffer_free")
        pool.reg_mov(rows_ready, ET)
        du_step = pool.alloc_register("du_step")
        deltas = pool.alloc_register("deltas")
        pool.reg_mov(buffer_free, PRIME - 2)
        pool.reg_mov(du_step, 1)
        pool.reg_mov(deltas, 1)
        inverse_root(0)
        times_u(0, 0, 0)
        with pool.Fori(0, B - 1) as b:
            main(b, b % 2, b + 1, (b + 1) % 2)
        main(B - 1, (B - 1) % 2, None, None)

    @block.vector
    def _(dve):
        dve.sem_inc(scan_done, PRIME)
        dve.sem_inc(hc_done, PRIME)
        dve.sem_inc(gated, PRIME)
        dve.sem_inc(x2_done, 1)
        dve.wait_ge(consts_in, 16 * 6)
        for t in range(ET):
            mk = dve.tensor_scalar(diag_d[:, t, :], ident[:], chan_sb[:, t, CD:CD + 1], None, ALU.mult)
        mk.then_inc(consts_made, 1)
        dve.wait_ge(a_exp, 2)
        dve.tensor_scalar(a_neg[:], a_neg[:], -1.0, None, ALU.mult).then_inc(signs_made, 1)

        def row_stats(b, t):
            if t == 0:
                dve.wait_ge(x_in, (b + 1) * 16)
            dve.bn_stats(stats[:, t, :], x2_all[:, at(b * LT + t), :]).then_inc(stats_done, 1)

        def row_aggr(b):
            dve.wait_ge(stats_done, rows_seen)
            dve.reg_add(rows_seen, rows_seen, ET)
            for t in range(ET):
                dve.bn_aggr(mean_var[:, t, :], stats[:, t, :]).then_inc(aggr_done, 1)

        def row_shift(b):
            dve.wait_ge(rstd_done, b + 1)
            dve.scalar_tensor_tensor(out=neg_mr[:], in0=mean_var[:, :, 0], scalar=-1.0, in1=rstd[:],
                                     op0=ALU.mult, op1=ALU.mult).then_inc(ln_done, 1)

        def conv(b, p, t, first=False):
            dve.wait_ge(tap_done, b * ET + t + 1)
            for s in range(1, DC):
                if s > 1:
                    dve.wait_ge(conv_step, b * 2 * ET + 2 * t + s - 1)
                w = chan_sb[:, t, CW + DC - 1 - s:CW + DC - s]
                acc = delta[:, at(p), t, s:]
                dve.scalar_tensor_tensor(out=acc, in0=(y_ps[:, t, 0:L - s] if first else proj[:, t % 2, 0:L - s]),
                                         scalar=w, in1=acc,
                                         op0=ALU.mult, op1=ALU.add).then_inc(conv_step if s < DC - 1 else conv_done, 1)

        def add_delta(b, p, t):
            dve.wait_ge(sp_ln, b + 1)
            dve.tensor_tensor(delta[:, at(p), t, :], delta[:, at(p), t, :], du[:, at(p), t, :], ALU.add)\
               .then_inc(delta_done, 1)

        def times_c(b, k):
            g, t, h, n = unit(k)
            if t == 0 and n == 0:
                dve.wait_ge(bc_in[h][1], b * 16 + 16)
            dve.wait_ge(scan_done, b * UNITS + k + 1 + PRIME)
            product = states[:, k % RING, :]
            dve.tensor_tensor(product, product, bc[:, h, 1, n, :], ALU.mult).then_inc(hc_done, 1)

        def gate_y(b, p, t):
            g = ET + t
            dve.wait_ge(acc_done, b * UNITS + HALF * (g + 1) + PRIME)
            dve.tensor_tensor(yz[:, t % 2, :], y_ps[:, t, :], sz[:, at(p), t, :], ALU.mult).then_inc(gated, 1)

        def residual(b, t):
            dve.wait_ge(turned_done, b * ET + t + 1)
            cols = x2_all[:, at(b * LT, LT), t * P:(t + 1) * P]
            dve.scalar_tensor_tensor(out=cols, in0=turned[:], scalar=gate[:, 0:1], in1=cols,
                                     op0=ALU.mult, op1=ALU.add).then_inc(x2_done, 1)

        def main(b, p, nb, np_):
            for k in range(UNITS):
                g, t, h, n = unit(k)
                dve.wait_ge(decay_done, b * UNITS + k + 1)
                if n % 2 == 0:
                    dve.wait_ge(dbu_done, b * (UNITS // 2) + k // 2 + 1)
                state = states[:, k % RING, :]
                dve.tensor_tensor_scan(state, state, dbu[:, k // 2 % 2, k % 2, :], 0.0,
                                       ALU.mult, ALU.add).then_inc(scan_done, 1)
                if k:
                    times_c(b, k - 1)
                if g > ET and n == 2:
                    gate_y(b, p, t - 1)
                if g > ET and n == 6:
                    residual(b, t - 1)
                if nb is not None:
                    if k < ET:
                        row_stats(nb, k)
                    if k == 6:
                        row_aggr(nb)
                    if k == 12:
                        row_shift(nb)
                    if k in CONV:
                        conv(nb, np_, CONV.index(k))
                    if k in DELTA:
                        add_delta(nb, np_, DELTA.index(k))
            times_c(b, UNITS - 1)
            gate_y(b, p, ET - 1)
            residual(b, ET - 1)

        rows_seen = dve.alloc_register("rows_seen")
        dve.reg_mov(rows_seen, ET)
        for t in range(ET):
            row_stats(0, t)
        row_aggr(0)
        row_shift(0)
        for t in range(ET):
            conv(0, 0, t, first=True)
        for t in range(ET):
            add_delta(0, 0, t)
        with dve.Fori(0, B - 1) as b:
            main(b, b % 2, b + 1, (b + 1) % 2)
        main(B - 1, (B - 1) % 2, None, None)


def moe_block(nc, ctx, x2_all, out, w_all, b_all, gate_wT, gate_b, consts, g_ffn, xs_dram, ys_dram):

    def sb(name, shape, dt=F32):
        return ctx.enter_context(nc.sbuf_tensor(name, shape, dt))

    def sem(name):
        return ctx.enter_context(nc.semaphore(name))

    def at(i, n=1):
        return bass.ds(i, n)

    cst = sb("cst", [P, CONSTS])
    ident, before, ones = cst[:, 0:P], cst[:, P:2 * P], cst[:, 2 * P:3 * P]
    same_expert, slot_no, preference = (cst[:, 3 * P:4 * P], cst[:, 4 * P:4 * P + SLOTS],
                                        cst[:, 4 * P + SLOTS:4 * P + SLOTS + E])
    gwT = sb("gwT", [P, HC, E])
    gb = sb("gb", [P, E])
    gate2 = sb("gate2", [P, 1])
    neg_half = sb("neg_half", [P, NT])
    st2 = sb("st2", [P, NT, 6])
    mv2 = sb("mv2", [P, NT, 2])
    rs2 = sb("rs2", [P, NT])
    nmr2 = sb("nmr2", [P, NT])
    logits = sb("logits", [P, NT, E])
    rest = sb("rest", [P, NT, E])
    first = sb("first", [P, NT, E])
    second = sb("second", [P, NT, E])
    tmp = sb("tmp", [P, NT, E])
    chosen = sb("chosen", [P, E, NT])
    top = sb("top", [P, 2, NT])
    pick = sb("pick", [P, NT])
    prob = sb("prob", [P, 2, NT])
    count = sb("count", [P, E, NT])
    rank = sb("rank", [P, E, NT])
    blocks_f = sb("blocks_f", [P, E])
    blocks_i = sb("blocks_i", [P, E], I32)
    ends_f = sb("ends_f", [P, E])
    ends_i = sb("ends_i", [P, E], I32)
    base = sb("base", [P, E])
    past = sb("past", [P, SLOTS, E])
    slot_f = sb("slot_f", [P, SLOTS])
    slot_expert = sb("slot_expert", [P, SLOTS], I32)
    pos_f = sb("pos_f", [P, 2, NT])
    pos = sb("pos", [P, 2, NT], U32)

    rows = sb("rows", [P, 4, H])
    inner = sb("inner", [P, 4, I])
    rowsT = inner[:].rearrange("p q (c t) -> p q c t", c=HC)
    glu, sig, lin, act_y = (inner[:, q, :] for q in range(4))

    stage = sb("stage", [P, WCOLS])
    w_hi = sb("w_hi", [P, 2, WCOLS], F32R)
    w_lo = sb("w_lo", [P, 2, WCOLS], F32R)
    bias = sb("bias", [P, 2, BCOLS])
    xT_hi = sb("xT_hi", [P, HC, P], F32R)
    xT_lo = sb("xT_lo", [P, HC, P], F32R)
    yT_hi = sb("yT_hi", [P, IC, P], F32R)
    yT_lo = sb("yT_lo", [P, IC, P], F32R)
    yo = sb("yo", [P, H])

    banks = ctx.enter_context(nc.psum_tensor("banks", [P, 4, 512], F32))
    xT_ps, yT_ps, glu_ps, lin_ps = (banks[:, q, :] for q in range(4))
    out_ps = ctx.enter_context(nc.psum_tensor("out_ps", [P, H], F32))
    lg_ps = ctx.enter_context(nc.psum_tensor("lg_ps", [P, NT, E], F32))
    rank_ps = ctx.enter_context(nc.psum_tensor("rank_ps", [P, E, NT], F32))
    count_ps = ctx.enter_context(nc.psum_tensor("count_ps", [P, E, NT], F32))

    cst_in = sem("cst_in")
    gate2_done = sem("gate2_done")
    powers = sem("powers")
    st2_done = sem("st2_done")
    mv2_done = sem("mv2_done")
    var2_eps = sem("var2_eps")
    rs2_done = sem("rs2_done")
    nmr2_done = sem("nmr2_done")
    rows_done = sem("rows_done")
    rows_turned = sem("rows_turned")
    rowsT_done = sem("rowsT_done")
    logits_mm = sem("logits_mm")
    route = sem("route")
    chosen_done = sem("chosen_done")
    diff_done = sem("diff_done")
    exp_done = sem("exp_done")
    ranks_mm = sem("ranks_mm")
    routed = sem("routed")
    rows_again = sem("rows_again")
    scattered = [sem(f"scattered{q}") for q in range(4)]
    w_in = sem("w_in")
    bias_in = sem("bias_in")
    hi_done = sem("hi_done")
    split_done = sem("split_done")
    xg_in = [sem(f"xg_in{q}") for q in range(2)]
    xT_mm = sem("xT_mm")
    xT_hi_done = sem("xT_hi_done")
    xT_lo_done = sem("xT_lo_done")
    glu_mm = sem("glu_mm")
    lin_mm = sem("lin_mm")
    glu_done = sem("glu_done")
    sig_done = sem("sig_done")
    lin_done = sem("lin_done")
    gs_done = sem("gs_done")
    act_done = sem("act_done")
    yT_mm = sem("yT_mm")
    yT_hi_done = sem("yT_hi_done")
    yT_lo_done = sem("yT_lo_done")
    out_mm = sem("out_mm")
    yo_done = sem("yo_done")
    ys_out = sem("ys_out")
    gathered = [sem(f"gathered{q}") for q in range(4)]
    combined = sem("combined")
    out_out = sem("out_out")

    block = ctx.enter_context(nc.Block())

    @block.sync
    def _(sp):
        sp.dma_start(cst[:], consts).then_inc(cst_in, 16)
        sp.dma_start(gwT[:], gate_wT).then_inc(cst_in, 16)
        sp.dma_start(gb[:], gate_b.to_broadcast([P, E])).then_inc(cst_in, 16)
        sp.dma_start(gate2[:], g_ffn.to_broadcast([P, 1])).then_inc(cst_in, 16)
        sp.sem_inc(ys_out, 16)
        for q in range(4):
            sp.wait_ge(scattered[q], 16 * 2 * NT // 4)
        def load_slot(s, q):
            sp.wait_ge(xT_mm, s - 1)
            sp.dma_start(rows[:, q, :], xs_dram[at(s * P, P), :]).then_inc(xg_in[q], 16)

        def store_slot(s):
            sp.wait_ge(yo_done, s + 1 + PRIME)
            sp.dma_start(ys_dram[at(s * P, P), :], yo[:]).then_inc(ys_out, 16)

        for q in range(2):
            sp.dma_start(rows[:, q, :], xs_dram[q * P:(q + 1) * P, :]).then_inc(xg_in[q], 16)
        load_slot(2, 0)
        with sp.Fori(0, PAIRS) as j:
            for q in range(2):
                s = j * 2 + q + 1
                load_slot(s + 2, 1 - q)
                store_slot(s - 1)
        for s in range(2 * PAIRS, SLOTS):
            store_slot(s)
        with sp.Fori(0, NT) as i:
            sp.wait_ge(combined, 2 * i + 2)
            sp.dma_start(out[at(i * P, P), :], x2_all[:, at(i), :].rearrange("p o d -> p (o d)")).then_inc(out_out, 16)
        sp.wait_ge(out_out, 16 * NT)

    @block.tensor
    def _(pe):
        pe.sem_inc(logits_mm, PRIME)
        pe.sem_inc(rows_turned, PRIME)
        pe.wait_ge(cst_in, 64)
        with pe.Fori(0, NT // 4) as j:
            for q in range(4):
                pe.wait_ge(rows_done, j * 4 + q + 1)
                pe.wait_ge(rowsT_done, j * 4 + q - 3 + PRIME)
                for c in range(HC):
                    mm = pe.transpose(banks[:, q, c * P:(c + 1) * P], rows[:, q, c * P:(c + 1) * P], ident)
                mm.then_inc(rows_turned, 1)
            for q in range(4):
                pe.wait_ge(rowsT_done, j * 4 + q + 1 + PRIME)
                for c in range(HC):
                    mm = pe.matmul(lg_ps[:, at(j * 4 + q), :], rowsT[:, q, c, :], gwT[:, c, :],
                                   start=c == 0, stop=c == HC - 1)
                mm.then_inc(logits_mm, 1)
        pe.wait_ge(chosen_done, 1)
        pe.matmul(rank_ps[:], before, chosen[:], start=True, stop=True)
        pe.matmul(count_ps[:], ones, chosen[:], start=True, stop=True).then_inc(ranks_mm, 1)

        def turn_x(s, q):
            pe.wait_ge(xg_in[q], (s - q) * 8 + 16)
            pe.wait_ge(xT_lo_done, s + PRIME)
            for c in range(HC):
                mm = pe.transpose(xT_ps[:, c * P:(c + 1) * P], rows[:, q, c * P:(c + 1) * P], ident)
            mm.then_inc(xT_mm, 1)

        def turn_y(s):
            pe.wait_ge(act_done, s + 1)
            pe.wait_ge(yT_lo_done, s + PRIME)
            for c in range(IC):
                mm = pe.transpose(yT_ps[:, c * P:(c + 1) * P], act_y[:, c * P:(c + 1) * P], ident)
            mm.then_inc(yT_mm, 1)

        def product(acc, hi, lo, chunks, par, col, width, done):
            for c in range(chunks):
                for n, (a, w) in enumerate(((hi, w_hi), (hi, w_lo), (lo, w_hi))):
                    cols = w[:, at(par), col + c * width:col + c * width + 512]
                    mm = pe.matmul(acc, a[:, c, :], cols.rearrange("p o n -> p (o n)"),
                                   start=c == 0 and n == 0, stop=c == chunks - 1 and n == 2)
            mm.then_inc(done, 1)

        def up(s, e, half):
            if half == 0:
                pe.wait_ge(split_done, e + 1)
                pe.wait_ge(xT_lo_done, s + 1 + PRIME)
                pe.wait_ge(glu_done, s + PRIME)
                product(glu_ps, xT_hi, xT_lo, HC, e % 2, 0, 2 * I, glu_mm)
            else:
                pe.wait_ge(lin_done, s + PRIME)
                product(lin_ps, xT_hi, xT_lo, HC, e % 2, I, 2 * I, lin_mm)

        def down(s, par):
            pe.wait_ge(yT_lo_done, s + 1 + PRIME)
            pe.wait_ge(yo_done, s + PRIME)
            product(out_ps[:], yT_hi, yT_lo, IC, par, HC * 2 * I, H, out_mm)

        def slot(s, q):
            e = pe.value_load(slot_expert[0:1, at(s)], min_val=0, max_val=E - 1)
            e_last = pe.value_load(slot_expert[0:1, at(s - 1)], min_val=0, max_val=E - 1)
            up(s, e, 0)
            turn_y(s - 1)
            up(s, e, 1)
            turn_x(s + 1, 1 - q)
            down(s - 1, e_last % 2)

        turn_x(0, 0)
        up(0, 0, 0)
        up(0, 0, 1)
        turn_x(1, 1)
        with pe.Fori(0, PAIRS) as j:
            for q in range(2):
                slot(j * 2 + q + 1, 1 - q)
        slot(SLOTS - 2, (SLOTS - 2) % 2)
        e = pe.value_load(slot_expert[0:1, SLOTS - 1:SLOTS], min_val=0, max_val=E - 1)
        e_last = pe.value_load(slot_expert[0:1, SLOTS - 2:SLOTS - 1], min_val=0, max_val=E - 1)
        up(SLOTS - 1, e, 0)
        turn_y(SLOTS - 2)
        up(SLOTS - 1, e, 1)
        down(SLOTS - 2, e_last % 2)
        turn_y(SLOTS - 1)
        down(SLOTS - 1, e % 2)

    @block.scalar
    def _(act):
        act.wait_ge(cst_in, 64)
        act.activation(gate2[:], gate2[:], ACT.Tanh).then_inc(gate2_done, 1)
        act.wait_ge(nmr2_done, 1)
        turned = act.alloc_register("turned")
        act.reg_mov(turned, PRIME - 3)
        with act.Fori(0, NT // 4) as j:
            for q in range(4):
                act.wait_ge(rows_turned, turned)
                act.reg_add(turned, turned, 1)
                act.activation(rows[:, q, :], x2_all[:, at(j * 4 + q), :], ACT.Identity,
                               scale=rs2[:, at(j * 4 + q)], bias=nmr2[:, at(j * 4 + q)]).then_inc(rows_done, 1)
        act.wait_ge(diff_done, 1)
        act.activation(prob[:, 1, :], prob[:, 1, :], ACT.Exp).then_inc(exp_done, 1)
        act.wait_ge(rows_turned, NT + PRIME)
        for i in range(NT):
            if i >= 4:
                act.wait_ge(scattered[i % 4], 32 * (i // 4))
            act.activation(rows[:, i % 4, :], x2_all[:, i, :], ACT.Identity,
                           scale=rs2[:, i:i + 1], bias=nmr2[:, i:i + 1]).then_inc(rows_again, 1)

        def keep_xT(s):
            act.wait_ge(xT_mm, s + 1)
            act.activation(xT_hi[:].rearrange("p c t -> p (c t)"), xT_ps, ACT.Copy).then_inc(xT_hi_done, 1)

        def sigmoid(s):
            act.wait_ge(glu_done, s + 1 + PRIME)
            act.activation(sig, glu, ACT.Sigmoid, scale=1.702).then_inc(sig_done, 1)

        def keep_yT(s):
            act.wait_ge(yT_mm, s + 1)
            act.activation(yT_hi[:].rearrange("p c t -> p (c t)"), yT_ps, ACT.Copy).then_inc(yT_hi_done, 1)

        keep_xT(0)
        sigmoid(0)
        keep_xT(1)
        with act.Fori(1, SLOTS - 1) as s:
            sigmoid(s)
            keep_yT(s - 1)
            keep_xT(s + 1)
        sigmoid(SLOTS - 1)
        keep_yT(SLOTS - 2)
        keep_yT(SLOTS - 1)

    @block.vector
    def _(dve):
        steps = [0]

        def step(ins):
            steps[0] += 1
            ins.then_inc(route, 1)
            dve.wait_ge(route, steps[0])

        dve.sem_inc(rowsT_done, PRIME)
        dve.sem_inc(xT_lo_done, PRIME)
        dve.sem_inc(yT_lo_done, PRIME)
        dve.sem_inc(glu_done, PRIME)
        dve.sem_inc(lin_done, PRIME)
        dve.sem_inc(yo_done, PRIME)
        for i in range(NT):
            dve.bn_stats(st2[:, i, :], x2_all[:, i, :]).then_inc(st2_done, 1)
        dve.wait_ge(st2_done, NT)
        for i in range(NT):
            dve.bn_aggr(mv2[:, i, :], st2[:, i, :]).then_inc(mv2_done, 1)
        dve.wait_ge(rs2_done, 1)
        dve.scalar_tensor_tensor(out=nmr2[:], in0=mv2[:, :, 0], scalar=-1.0, in1=rs2[:],
                                 op0=ALU.mult, op1=ALU.mult).then_inc(nmr2_done, 1)
        with dve.Fori(0, NT // 4) as j:
            for q in range(4):
                dve.wait_ge(logits_mm, j * 4 + q - 3 + PRIME)
                dve.wait_ge(rows_turned, j * 4 + q + 1 + PRIME)
                dve.tensor_copy(rowsT[:, q, :, :].rearrange("p c t -> p (c t)"), banks[:, q, :])\
                   .then_inc(rowsT_done, 1)
        dve.wait_ge(logits_mm, NT + PRIME)

        def per_row(a):
            return a.unsqueeze(2).to_broadcast([P, NT, E])

        def per_expert(a, n=NT):
            return a.unsqueeze(1).to_broadcast([P, n, E])

        def choose(scores, value, onehot):
            step(dve.tensor_reduce(value, scores, AX.X, ALU.max))
            step(dve.tensor_tensor(tmp[:], scores, per_row(value), ALU.is_equal))
            step(dve.tensor_tensor(tmp[:], tmp[:], per_expert(preference), ALU.mult))
            step(dve.tensor_reduce(pick[:], tmp[:], AX.X, ALU.max))
            step(dve.tensor_tensor(onehot, per_expert(preference), per_row(pick[:]), ALU.is_equal))

        step(dve.tensor_tensor(logits[:], lg_ps[:], per_expert(gb[:]), ALU.add))
        choose(logits[:], top[:, 0, :], first[:])
        step(dve.scalar_tensor_tensor(out=rest[:], in0=first[:], scalar=-3.0e38, in1=logits[:],
                                      op0=ALU.mult, op1=ALU.add))
        choose(rest[:], top[:, 1, :], second[:])
        dve.tensor_tensor(chosen[:].rearrange("p e i -> p i e"), first[:], second[:], ALU.add).then_inc(chosen_done, 1)
        dve.tensor_tensor(prob[:, 1, :], top[:, 1, :], top[:, 0, :], ALU.subtract).then_inc(diff_done, 1)
        dve.wait_ge(ranks_mm, 1)
        flat = "p e i -> p (e i)"
        step(dve.tensor_tensor_scan(count[:].rearrange(flat), same_expert, count_ps[:].rearrange(flat), 0.0,
                                    ALU.mult, ALU.add))
        step(dve.tensor_scalar(blocks_f[:], count[:, :, NT - 1], 1.0, float(P - 1), ALU.max, ALU.add))
        step(dve.tensor_copy(blocks_i[:], blocks_f[:]))
        step(dve.tensor_scalar(blocks_i[:], blocks_i[:], 7, None, ALU.arith_shift_right))
        step(dve.tensor_copy(blocks_f[:], blocks_i[:]))
        step(dve.tensor_tensor_scan(ends_f[:], ones[:, 0:E], blocks_f[:], 0.0, ALU.mult, ALU.add))
        dve.tensor_copy(ends_i[:], ends_f[:])
        step(dve.tensor_tensor(base[:], ends_f[:], blocks_f[:], ALU.subtract))
        step(dve.tensor_scalar(base[:], base[:], float(P), None, ALU.mult))
        step(dve.tensor_tensor(rank[:], count[:], count_ps[:], ALU.subtract))
        step(dve.tensor_tensor(rank[:], rank[:], rank_ps[:], ALU.add))
        step(dve.tensor_tensor(rank[:], rank[:], base[:].unsqueeze(2).to_broadcast([P, E, NT]), ALU.add))
        for r, onehot in enumerate((first, second)):
            step(dve.tensor_tensor(tmp[:], onehot[:], rank[:].rearrange("p e i -> p i e"), ALU.mult))
            step(dve.tensor_reduce(pos_f[:, r, :], tmp[:], AX.X, ALU.add))
        step(dve.tensor_copy(pos[:], pos_f[:]))
        step(dve.tensor_tensor(past[:], slot_no.unsqueeze(2).to_broadcast([P, SLOTS, E]),
                               per_expert(ends_f[:], SLOTS), ALU.is_ge))
        step(dve.tensor_reduce(slot_f[:], past[:], AX.X, ALU.add))
        step(dve.tensor_scalar(slot_f[:], slot_f[:], float(E - 1), None, ALU.min))
        dve.tensor_copy(slot_expert[:], slot_f[:]).then_inc(routed, 1)
        dve.wait_ge(exp_done, 1)
        step(dve.tensor_scalar(pick[:], prob[:, 1, :], 1.0, None, ALU.add))
        step(dve.reciprocal(prob[:, 0, :], pick[:]))
        dve.wait_ge(gate2_done, 1)
        step(dve.tensor_scalar(prob[:, 0, :], prob[:, 0, :], gate2[:, 0:1], None, ALU.mult))
        step(dve.tensor_tensor(prob[:, 1, :], prob[:, 1, :], prob[:, 0, :], ALU.mult))

        def rest_of_xT(s):
            dve.wait_ge(xT_hi_done, s + 1)
            dve.tensor_tensor(xT_lo[:].rearrange("p c t -> p (c t)"), xT_ps,
                              xT_hi[:].rearrange("p c t -> p (c t)").bitcast(F32), ALU.subtract).then_inc(xT_lo_done, 1)

        def glu_bias(s, par):
            dve.wait_ge(glu_mm, s + 1)
            dve.tensor_tensor(glu, glu_ps, bias[:, at(par), 0:I].rearrange("p o n -> p (o n)"), ALU.add)\
               .then_inc(glu_done, 1)

        def activate(s, par):
            dve.wait_ge(sig_done, s + 1)
            dve.tensor_tensor(sig, glu, sig, ALU.mult).then_inc(gs_done, 1)
            dve.wait_ge(lin_mm, s + 1)
            dve.scalar_tensor_tensor(out=lin, in0=lin_ps, scalar=1.0, op0=ALU.add, op1=ALU.add,
                                     in1=bias[:, at(par), I:2 * I].rearrange("p o n -> p (o n)"))\
               .then_inc(lin_done, 1)
            dve.wait_ge(gs_done, s + 1)
            dve.wait_ge(lin_done, s + 1 + PRIME)
            dve.tensor_tensor(act_y, sig, lin, ALU.mult).then_inc(act_done, 1)

        def rest_of_yT(s):
            dve.wait_ge(yT_hi_done, s + 1)
            dve.tensor_tensor(yT_lo[:].rearrange("p c t -> p (c t)"), yT_ps,
                              yT_hi[:].rearrange("p c t -> p (c t)").bitcast(F32), ALU.subtract).then_inc(yT_lo_done, 1)

        def keep_out(s, par):
            dve.wait_ge(out_mm, s + 1)
            dve.wait_ge(ys_out, s * 16 + 16)
            dve.tensor_tensor(yo[:], out_ps[:], bias[:, at(par), 2 * I:].rearrange("p o n -> p (o n)"), ALU.add)\
               .then_inc(yo_done, 1)

        dve.wait_ge(routed, 1)
        rest_of_xT(0)
        dve.wait_ge(bias_in, 16)
        glu_bias(0, 0)
        rest_of_xT(1)
        activate(0, 0)
        with dve.Fori(1, SLOTS - 1) as s:
            e = dve.value_load(slot_expert[0:1, at(s)], min_val=0, max_val=E - 1)
            e_last = dve.value_load(slot_expert[0:1, at(s - 1)], min_val=0, max_val=E - 1)
            dve.wait_ge(bias_in, e * 16 + 16)
            glu_bias(s, e % 2)
            rest_of_yT(s - 1)
            rest_of_xT(s + 1)
            activate(s, e % 2)
            keep_out(s - 1, e_last % 2)
        e = dve.value_load(slot_expert[0:1, SLOTS - 1:SLOTS], min_val=0, max_val=E - 1)
        e_last = dve.value_load(slot_expert[0:1, SLOTS - 2:SLOTS - 1], min_val=0, max_val=E - 1)
        glu_bias(SLOTS - 1, e % 2)
        rest_of_yT(SLOTS - 2)
        activate(SLOTS - 1, e % 2)
        keep_out(SLOTS - 2, e_last % 2)
        rest_of_yT(SLOTS - 1)
        keep_out(SLOTS - 1, e % 2)
        for n in range(2 * NT):
            i, r = n // 2, n % 2
            dve.wait_ge(gathered[n % 4], 16 * (n // 4 + 1))
            if r:
                dve.wait_ge(combined, n)
            dve.scalar_tensor_tensor(out=x2_all[:, i, :], in0=rows[:, n % 4, :], scalar=prob[:, r, i:i + 1],
                                     in1=x2_all[:, i, :], op0=ALU.mult, op1=ALU.add).then_inc(combined, 1)

    @block.gpsimd
    def _(pool):
        pool.memset(neg_half[:], -0.5).then_inc(powers, 1)

        def load_expert(e):
            pool.dma_start(stage[:], w_all[at(e), :, :].rearrange("o p n -> p (o n)")).then_inc(w_in, 16)

        def split_expert(e, par):
            pool.dma_start(bias[:, par, :], b_all[at(e), :].to_broadcast([P, BCOLS])).then_inc(bias_in, 16)
            pool.wait_ge(w_in, loaded)
            pool.reg_add(loaded, loaded, 16)
            pool.tensor_scalar(w_hi[:, par, :], stage[:], 1.0, 1.0, ALU.mult, ALU.mult).then_inc(hi_done, 1)
            pool.wait_ge(hi_done, e + 1)
            pool.tensor_tensor(w_lo[:, par, :], stage[:], w_hi[:, par, :].bitcast(F32), ALU.subtract)\
                .then_inc(split_done, 1)
            pool.wait_ge(bias_in, e * 16 + 16)

        pool.wait_ge(powers, 1)
        pool.wait_ge(mv2_done, NT)
        pool.tensor_scalar(rs2[:], mv2[:, :, 1], EPS, 1.0, ALU.add, ALU.mult).then_inc(var2_eps, 1)
        pool.wait_ge(var2_eps, 1)
        pool.tensor_tensor(rs2[:], rs2[:], neg_half[:], ALU.pow).then_inc(rs2_done, 1)
        loaded = pool.alloc_register("loaded")
        pool.reg_mov(loaded, 16)
        load_expert(0)
        split_expert(0, 0)
        pool.wait_ge(split_done, 1)
        load_expert(1)
        pool.wait_ge(routed, 1)
        for n in range(2 * NT):
            i, r = n // 2, n % 2
            pool.wait_ge(rows_again, i + 1)
            pool.indirect_dma_start(out=xs_dram, out_offset=bass.IndirectOffsetOnAxis(ap=pos[:, r, i:i + 1], axis=0),
                                    in_=rows[:, i % 4, :], in_offset=None).then_inc(scattered[i % 4], 16)
        split_expert(1, 1)
        with pool.Fori(1, E // 2) as j:
            for q in range(2):
                e = j * 2 + q
                pool.wait_ge(split_done, e)
                load_expert(e)
                end = pool.value_load(ends_i[0:1, at(e - 2)], min_val=1, max_val=SLOTS)
                pool.wait_ge(yo_done, end + PRIME)
                split_expert(e, q)
        pool.wait_ge(ys_out, 16 * SLOTS + 16)
        for n in range(2 * NT):
            i, r = n // 2, n % 2
            if n >= 4:
                pool.wait_ge(combined, n - 3)
            pool.indirect_dma_start(out=rows[:, n % 4, :], out_offset=None, in_=ys_dram,
                                    in_offset=bass.IndirectOffsetOnAxis(ap=pos[:, r, i:i + 1], axis=0))\
                .then_inc(gathered[n % 4], 16)



def build(nc, x, ctxT, inT, chan, xprojT, dtT, g_x, w_all, b_all, gate_wT, gate_b, g_ffn, consts, out):
    with ExitStack() as whole:
        x2_all = whole.enter_context(nc.sbuf_tensor("x2_all", [P, NT, H], F32))
        bc_dram = nc.dram_tensor("bc_dram", [B, 2 * DS, L], F32, kind="Internal").ap()
        xs_dram = nc.dram_tensor("xs_dram", [SLOTS * P, H], F32, kind="Internal").ap()
        ys_dram = nc.dram_tensor("ys_dram", [SLOTS * P, H], F32, kind="Internal").ap()
        with ExitStack() as ctx:
            mamba_block(nc, ctx, x2_all, x, ctxT, inT, chan, xprojT, dtT, consts[:, 0:P], g_x, bc_dram, xs_dram)
        with ExitStack() as ctx:
            moe_block(nc, ctx, x2_all, out.rearrange("b l d -> (b l) d"), w_all, b_all, gate_wT, gate_b, consts,
                      g_ffn, xs_dram, ys_dram)


def kernel(**inputs):
    from concourse import bacc
    from concourse.bass_utils import run_bass_kernel_spmd

    a = {k: np.asarray(v) for k, v in inputs.items()}

    def rows(w, chunks):
        return w.reshape(chunks, P, -1).transpose(1, 0, 2)

    chan = np.concatenate([rows(a["L0_xattn_" + n], ET) for n in ("conv_w", "conv_b", "D", "dt_proj_b", "A_log")], 2)
    w1 = a["L0_ffn_w1"].reshape(E, I, 2, H).transpose(0, 3, 2, 1).reshape(E, HC, P, 2 * I)
    w2 = a["L0_ffn_w2"].transpose(0, 2, 1).reshape(E, IC, P, H)
    w_all = np.concatenate([w.transpose(0, 2, 1, 3).reshape(E, P, -1) for w in (w1, w2)], 2)
    b1 = a["L0_ffn_b1"].reshape(E, I, 2).transpose(0, 2, 1).reshape(E, 2 * I)
    consts = np.concatenate([np.eye(P), np.triu(np.ones((P, P)), 1), np.ones((P, P)),
                             np.tile(np.arange(P) % NT > 0, (P, 1)), np.tile(np.arange(SLOTS), (P, 1)),
                             np.tile(E - np.arange(E), (P, 1))], 1).astype(np.float32)
    arrays = {
        "x": a["x"],
        "ctxT": a["ctx_1024"].transpose(0, 2, 1).reshape(B, KC, P, L),
        "inT": rows(a["L0_xattn_in_proj_w"].T, KC),
        "chan": chan,
        "xprojT": rows(a["L0_xattn_x_proj_w"].T, ET),
        "dtT": a["L0_xattn_dt_proj_w"].T,
        "g_x": a["g_xattn"].reshape(1, 1),
        "w_all": w_all,
        "b_all": np.concatenate([b1, a["L0_ffn_b2"]], 1),
        "gate_wT": rows(a["L0_ffn_gate_w"].T, HC),
        "gate_b": a["L0_ffn_gate_b"].reshape(1, E),
        "g_ffn": a["g_ffn"].reshape(1, 1),
        "consts": consts,
    }
    arrays = {k: np.ascontiguousarray(v) for k, v in arrays.items()}
    nc = bacc.Bacc("TRN2", target_bir_lowering=False, num_devices=1)
    args = [nc.dram_tensor(k, v.shape, F32, kind="ExternalInput").ap() for k, v in arrays.items()]
    out = nc.dram_tensor("out", (B, L, H), F32, kind="ExternalOutput").ap()
    build(nc, *args, out)
    got = run_bass_kernel_spmd(nc, [arrays], core_ids=[0])
    return got.results[0]["out"]
```

```python
from contextlib import ExitStack

import numpy as np

import concourse.bass as bass
from concourse import mybir

F32 = mybir.dt.float32
F32R = mybir.dt.float32r
I32 = mybir.dt.int32
U32 = mybir.dt.uint32
AX = mybir.AxisListType
ALU = mybir.AluOpType
ACT = mybir.ActivationFunctionType

P = 128
B, L, DM = 4, 512, 256
DI, DS, DR, DC = 512, 16, 16, 4
ET = DI // P
LT = L // P
KC = DM // P
HALF = DS // 2
UNITS = ET * DS
EPS = 1e-5
H, I, E, TOP = 512, 512, 8, 2
HC, IC = H // P, I // P
NT = B * LT
SLOTS = (TOP * NT * P + E * P - 1) // P
PAIRS = (SLOTS - 3) // 2
assert SLOTS == 2 * PAIRS + 3
LOW_EARLY, LOW_AHEAD = 4, 10
WCOLS = HC * 2 * I + IC * H
BCOLS = 2 * I + H
EARLY = (B - 1) * LT
REGION = NT * P + P
CONSTS = 3 * P + E * NT + SLOTS + 2 * E
CW, CB, CD, CDT, CA = 0, DC, DC + 1, DC + 2, DC + 3
NCH = DC + 3 + DS

PRIME = 8
PAIR_RING = 4
RING = 8


SUMMED = (1, 3)
TAPPED = tuple(t for t in range(ET) if t not in SUMMED)
IN_PROJ, TAP, CONV, KEEP_CONV = (1, 6, 12, 18), (10, 15, 21, 27), (8, 14, 20, 25), (24, 33)
GATE_SILU, U_SILU = 6, 34
STATS, STATS_AGGR, STATS_ROOT, STATS_SHIFT = 26, 34, 38, 40
X_PROJ, KEEP_XD = (31, 32, 33, 34), 43
DELTA_PROJ, SOFTPLUS, SOFTPLUS_EXP, DELTA = (37, 39, 42, 45), (46, 48, 53, 54), 55, (56, 59, 60, 62)

TILES_A_UNIT = 3
ROOT_LATE = 8
AGGR, ROOT, SHIFT = EARLY // TILES_A_UNIT + 1, 14, 11
ROW, TURN, KEEP_TURNED, LOGIT = (range(k, k + 2 * EARLY, 2) for k in (16, 12, 21, 19))
CHOOSE, RANK_SUMS, RANKS = (46, 47), 50, 53


def unit(k):
    g = k // HALF
    return g, g % ET, g // ET, k % HALF

WARM_START, WARM_CONV, WARM_MAIN, WARM_ROUTER, WARM_SLOTS = 3, 10, 6, 4, 12


def keep_warm(pe, n, bank, lhsT, rhs):
    for _ in range(n):
        pe.matmul(bank, lhsT, rhs, start=True, stop=True)


class Named:
    pass


def routing_buffers(nc, ctx):

    def sb(name, shape, dt=F32):
        return ctx.enter_context(nc.sbuf_tensor(name, shape, dt))

    R = Named()
    R.cst = sb("cst", [P, CONSTS])
    R.ident, R.before, R.ones = (R.cst[:, i * P:(i + 1) * P] for i in range(3))
    at = 3 * P
    R.later_tile = []
    for n in (EARLY, NT - EARLY):
        R.later_tile.append(R.cst[:, at:at + E * n])
        at += E * n
    R.slot_no = R.cst[:, at:at + SLOTS]
    R.preference = R.cst[:, at + SLOTS:at + SLOTS + E]
    R.region = R.cst[:, at + SLOTS + E:at + SLOTS + 2 * E]
    R.gwT = sb("gwT", [P, HC, E])
    R.gb = sb("gb", [P, E])
    R.neg_half = sb("neg_half", [P, NT])
    R.st = sb("st2", [P, NT, 6])
    R.mv = sb("mv2", [P, NT, 2])
    R.rs = sb("rs2", [P, NT])
    R.nmr = sb("nmr2", [P, NT])
    R.top = sb("top", [P, 2, NT])
    R.pos_f = sb("pos_f", [P, 2, NT])
    R.pos_x = sb("pos_x", [P, 2, NT], U32)
    R.groups = []
    for g, (lo, hi) in enumerate(((0, EARLY), (EARLY, NT))):
        G = Named()
        G.lo, G.hi, G.n = lo, hi, hi - lo
        G.later_tile = R.later_tile[g]
        G.logits = sb(f"logits{g}", [P, G.n, E])
        G.onehot = [sb(f"onehot{g}{r}", [P, G.n, E]) for r in range(2)]
        G.tmp = R.groups[0].tmp[:, 0:G.n, :] if g else sb("tmp", [P, G.n, E])
        G.chosen = sb(f"chosen{g}", [P, E, G.n])
        G.pick = sb(f"pick{g}", [P, G.n])
        G.count = sb(f"count{g}", [P, E, G.n])
        G.rank = G.chosen
        R.groups.append(G)
    R.st_done = ctx.enter_context(nc.semaphore("st_done"))
    R.mv_done = ctx.enter_context(nc.semaphore("mv_done"))
    R.var_eps2 = ctx.enter_context(nc.semaphore("var_eps2"))
    R.rs_done = ctx.enter_context(nc.semaphore("rs_done"))
    R.nmr_done = ctx.enter_context(nc.semaphore("nmr_done"))
    R.rows_done = ctx.enter_context(nc.semaphore("rows_done"))
    R.rows_turned = ctx.enter_context(nc.semaphore("rows_turned"))
    R.rowsT_done = ctx.enter_context(nc.semaphore("rowsT_done"))
    R.logits_mm = ctx.enter_context(nc.semaphore("logits_mm"))
    R.route = ctx.enter_context(nc.semaphore("route"))
    R.chosen_done = ctx.enter_context(nc.semaphore("chosen_done"))
    R.ranks_mm = ctx.enter_context(nc.semaphore("ranks_mm"))
    R.pos_done = ctx.enter_context(nc.semaphore("pos_done"))
    R.scattered = ctx.enter_context(nc.semaphore("scattered"))
    R.w_first = ctx.enter_context(nc.semaphore("w_first"))
    R.router_in = ctx.enter_context(nc.semaphore("router_in"))
    R.steps = 0
    return R


def step(dve, R, ins):
    R.steps += 1
    ins.then_inc(R.route, 1)
    dve.wait_ge(R.route, R.steps)


def choose(dve, R, G, r, logits_ps):

    def per_row(a):
        return a.unsqueeze(2).to_broadcast([P, G.n, E])

    def per_expert(a):
        return a.unsqueeze(1).to_broadcast([P, G.n, E])

    scores, value, tmp, pick = G.logits[:], R.top[:, r, G.lo:G.hi], G.tmp[:], G.pick[:]
    if r == 0:
        dve.wait_ge(R.logits_mm, G.hi)
        dve.wait_ge(R.router_in, 32)
        step(dve, R, dve.tensor_tensor(scores, logits_ps, per_expert(R.gb[:]), ALU.add))
    else:
        step(dve, R, dve.scalar_tensor_tensor(out=scores, in0=G.onehot[0][:], scalar=-3.0e38, in1=scores,
                                              op0=ALU.mult, op1=ALU.add))
    step(dve, R, dve.tensor_reduce(value, scores, AX.X, ALU.max))
    step(dve, R, dve.tensor_tensor(tmp, scores, per_row(value), ALU.is_equal))
    step(dve, R, dve.tensor_tensor(tmp, tmp, per_expert(R.preference), ALU.mult))
    step(dve, R, dve.tensor_reduce(pick, tmp, AX.X, ALU.max))
    step(dve, R, dve.tensor_tensor(G.onehot[r][:], per_expert(R.preference), per_row(pick), ALU.is_equal))
    if r == 1:
        dve.tensor_tensor(G.chosen[:].rearrange("p e i -> p i e"), G.onehot[0][:], G.onehot[1][:], ALU.add)\
           .then_inc(R.chosen_done, 1)


def rank_sums(pe, R, G, g, rank_ps, count_ps):
    pe.wait_ge(R.chosen_done, g + 1)
    pe.matmul(rank_ps, R.before, G.chosen[:], start=True, stop=True)
    pe.matmul(count_ps, R.ones, G.chosen[:], start=True, stop=True).then_inc(R.ranks_mm, 1)


def places(dve, R, G, g, rank_ps, count_ps):
    flat = "p e i -> p (e i)"

    def per_tile(a):
        return a.unsqueeze(2).to_broadcast([P, E, G.n])

    dve.wait_ge(R.ranks_mm, g + 1)
    step(dve, R, dve.tensor_tensor_scan(G.count[:].rearrange(flat), G.later_tile, count_ps.rearrange(flat), 0.0,
                                        ALU.mult, ALU.add))
    if g:
        before = R.groups[g - 1].count[:, :, R.groups[g - 1].n - 1]
        step(dve, R, dve.tensor_tensor(G.count[:], G.count[:], per_tile(before), ALU.add))
    step(dve, R, dve.tensor_tensor(G.rank[:], G.count[:], count_ps, ALU.subtract))
    step(dve, R, dve.tensor_tensor(G.rank[:], G.rank[:], rank_ps, ALU.add))
    step(dve, R, dve.tensor_tensor(G.rank[:], G.rank[:], per_tile(R.region), ALU.add))
    for r in range(2):
        step(dve, R, dve.tensor_tensor(G.tmp[:], G.onehot[r][:], G.rank[:].rearrange("p e i -> p i e"), ALU.mult))
        step(dve, R, dve.tensor_reduce(R.pos_f[:, r, G.lo:G.hi], G.tmp[:], AX.X, ALU.add))
    dve.tensor_copy(R.pos_x[:, :, G.lo:G.hi], R.pos_f[:, :, G.lo:G.hi]).then_inc(R.pos_done, 1)


def row_roots(pool, R, G, g):
    pool.wait_ge(R.mv_done, G.hi)
    pool.tensor_scalar(R.rs[:, G.lo:G.hi], R.mv[:, G.lo:G.hi, 1], EPS, 1.0, ALU.add, ALU.mult).then_inc(R.var_eps2, 1)
    pool.wait_ge(R.var_eps2, g + 1)
    pool.tensor_tensor(R.rs[:, G.lo:G.hi], R.rs[:, G.lo:G.hi], R.neg_half[:, G.lo:G.hi], ALU.pow)\
        .then_inc(R.rs_done, 1)


def row_shifts(dve, R, G, g):
    dve.wait_ge(R.rs_done, g + 1)
    dve.scalar_tensor_tensor(out=R.nmr[:, G.lo:G.hi], in0=R.mv[:, G.lo:G.hi, 0], scalar=-1.0,
                             in1=R.rs[:, G.lo:G.hi], op0=ALU.mult, op1=ALU.mult).then_inc(R.nmr_done, 1)


def scatter_rows(pool, R, i, row, xs_dram):
    pool.wait_ge(R.rows_done, i + 1)
    for r in range(2):
        pool.indirect_dma_start(out=xs_dram, out_offset=bass.IndirectOffsetOnAxis(ap=R.pos_x[:, r, i:i + 1], axis=0),
                                in_=row, in_offset=None).then_inc(R.scattered, 16)


def mamba_block(nc, ctx, R, shared, x2_all, x, ctxT, inT, chan, xprojT, dtT, consts, gate_wT, gate_b, g_x, bc_dram,
                xs_dram, ys_dram, w_all):

    def sb(name, shape, dt=F32):
        return ctx.enter_context(nc.sbuf_tensor(name, shape, dt))

    def sem(name):
        return ctx.enter_context(nc.semaphore(name))

    ctx_sb = sb("ctx_sb", [P, KC, L])
    inT_sb = sb("inT_sb", [P, KC, DI])
    chan_sb = sb("chan_sb", [P, ET, NCH])
    a_neg = chan_sb[:, :, CA:CA + DS]
    xprojT_sb = sb("xprojT_sb", [P, ET, DR + 2 * DS])
    dtT_sb = sb("dtT_sb", [DR, DI])
    ident = R.ident
    diag_d = sb("diag_d", [P, ET, P])
    gate = sb("gate", [P, 1])
    half_pow = sb("half_pow", [P, ET])
    stats = sb("stats", [P, ET, 6])
    mean_var = sb("mean_var", [P, ET, 2])
    rstd = sb("rstd", [P, ET])
    neg_mr = sb("neg_mr", [P, ET])
    u = sb("u", [P, ET, L])
    delta = sb("delta", [P, 2, ET, L])
    du = sb("du", [P, 2, ET, L])
    sz = sb("sz", [P, ET, L])
    diag_w = sb("diag_w", [P, ET, DC, P])
    xd = sb("xd", [DR + 2 * DS, L])
    bc = shared[:].rearrange("p (h s n l) -> p h s n l", h=2, s=2, n=HALF)
    dbu = sb("dbu", [P, PAIR_RING, 2, L])
    states = sb("states", [P, RING, L])
    yz = sb("yz", [P, L])
    early = R.groups[0]
    row_buf = [buf[:, B % 2, t, :] for buf in (delta, du) for t in range(ET)]
    row_buf += [diag_w[:, t, :, :].rearrange("p s c -> p (s c)") for t in range(ET)]
    rowT_buf = [ctx_sb[:, c, :] for c in range(KC)]
    late = R.groups[1]
    late_row, late_rowT = (shared[:, WCOLS + q * 4 * H:WCOLS + (q + 1) * 4 * H].rearrange("p (i h) -> p i h", i=4)
                           for q in range(2))

    y_ps = ctx.enter_context(nc.psum_tensor("y_ps", [P, ET, L], F32))
    proj = ctx.enter_context(nc.psum_tensor("proj", [P, 2, L], F32))
    turned = ctx.enter_context(nc.psum_tensor("turned", [P, LT, P], F32))
    assert 0 not in SUMMED
    zeros = diag_w[:, 0, :, :].rearrange("p s c -> p (s c)")
    conv_ps = ctx.enter_context(nc.psum_tensor("conv_ps", [P, L], F32))
    route_ps = conv_ps[:, 0:3 * EARLY * E].rearrange("p (q n) -> p q n", q=3)
    late_ps = conv_ps[:, 3 * EARLY * E:3 * NT * E].rearrange("p (q n) -> p q n", q=3)
    late_logits_ps = late_ps[:, 0, :].rearrange("p (i e) -> p i e", e=E)
    late_rank_ps, late_count_ps = (late_ps[:, q, :].rearrange("p (e i) -> p e i", e=E) for q in (1, 2))
    logits_ps = route_ps[:, 0, :].rearrange("p (i e) -> p i e", e=E)
    rank_ps, count_ps = (route_ps[:, q, :].rearrange("p (e i) -> p e i", e=E) for q in (1, 2))

    yz_cleared = sem("yz_cleared")
    inT_in = sem("inT_in")
    zeros_made = sem("zeros_made")
    ys_cleared = sem("ys_cleared")
    consts_in = sem("consts_in")
    consts_made = sem("consts_made")
    signs_made = sem("signs_made")
    pows_made = sem("pows_made")
    a_exp = sem("a_exp")
    x_in = sem("x_in")
    ctx_in = sem("ctx_in")
    xs_out = sem("xs_out")
    bc_in = [[sem(f"{name}_in{h}") for name in ("b", "c")] for h in range(2)]
    stats_done = sem("stats_done")
    aggr_done = sem("aggr_done")
    var_eps = sem("var_eps")
    rstd_done = sem("rstd_done")
    ln_done = sem("ln_done")
    inproj_done = sem("inproj_done")
    tap_done = sem("tap_done")
    conv_step = sem("conv_step")
    conv_mm = sem("conv_mm")
    conv_kept = sem("conv_kept")
    conv_done = sem("conv_done")
    u_done = sem("u_done")
    sz_done = sem("sz_done")
    xd_mm = sem("xd_mm")
    xd_done = sem("xd_done")
    delta_mm = sem("delta_mm")
    sp_read = sem("sp_read")
    relu_done = sem("relu_done")
    sp_exp = sem("sp_exp")
    sp_ln = sem("sp_ln")
    delta_done = sem("delta_done")
    du_done = sem("du_done")
    decay_done = sem("decay_done")
    dbu_done = sem("dbu_done")
    scan_done = sem("scan_done")
    hc_done = sem("hc_done")
    acc_done = sem("acc_done")
    gated = sem("gated")
    turned_done = sem("turned_done")
    x2_done = sem("x2_done")

    def at(i, n=1):
        return bass.ds(i, n)

    block = ctx.enter_context(nc.Block())

    @block.sync
    def _(sp):
        sp.dma_start(inT_sb[:], inT).then_inc(inT_in, 16)

        def load_ctx(b):
            sp.wait_ge(inproj_done, ET * b + PRIME)
            sp.dma_start(ctx_sb[:], ctxT[at(b), :, :, :].rearrange("o k p l -> p (o k) l")).then_inc(ctx_in, 16)

        def load_x(b):
            sp.dma_start(x2_all[:, at(b * LT, LT), :], x[at(b), :, :].rearrange("o (t p) d -> p (o t) d", p=P))\
              .then_inc(x_in, 16)

        def store_bc(b):
            sp.wait_ge(xd_done, b + 1)
            sp.dma_start(bc_dram[at(b), :, :], xd[DR:, :]).then_inc(xs_out, 16)
            sp.wait_ge(xs_out, (b + 1) * 16)

        def spread_half(b, h, first=False):
            if not first:
                sp.wait_ge(hc_done, b * UNITS + PRIME - (UNITS // 2) * (1 - h))
            for s in range(2):
                rows = bc_dram[at(b), s * DS + h * HALF:s * DS + (h + 1) * HALF, :]
                sp.dma_start(bc[:, h, s, :, :].rearrange("p n l -> p (n l)"),
                             rows.rearrange("o n l -> o (n l)").to_broadcast([P, HALF * L])).then_inc(bc_in[h][s], 16)

        load_ctx(0)
        sp.dma_start(chan_sb[:], chan).then_inc(consts_in, 16)
        sp.dma_start(R.cst[:], consts).then_inc(consts_in, 16)
        sp.dma_start(xprojT_sb[:], xprojT).then_inc(consts_in, 16)
        sp.dma_start(dtT_sb[:], dtT).then_inc(consts_in, 16)
        sp.dma_start(gate[:], g_x.to_broadcast([P, 1])).then_inc(consts_in, 16)
        load_x(0)
        sp.dma_start(R.gwT[:], gate_wT).then_inc(R.router_in, 16)
        sp.dma_start(R.gb[:], gate_b.to_broadcast([P, E])).then_inc(R.router_in, 16)
        store_bc(0)
        spread_half(0, 0, first=True)
        sp.wait_ge(x_in, 16)
        load_ctx(1)
        load_x(1)
        spread_half(0, 1, first=True)
        sp.wait_ge(zeros_made, 1)
        sp.dma_start(ys_dram.rearrange("(s p) d -> p s d", p=P), zeros.unsqueeze(1).to_broadcast([P, SLOTS, H]))\
          .then_inc(ys_cleared, 16)
        with sp.Fori(1, B - 1) as b:
            store_bc(b)
            spread_half(b, 0)
            sp.wait_ge(x_in, b * 16 + 16)
            load_ctx(b + 1)
            load_x(b + 1)
            spread_half(b, 1)
        store_bc(B - 1)
        spread_half(B - 1, 0)
        spread_half(B - 1, 1)
        sp.wait_ge(hc_done, (B - 1) * UNITS + UNITS // 2 + PRIME)
        sp.dma_start(shared[:, 0:WCOLS], w_all[0, :, :]).then_inc(R.w_first, 16)
        sp.wait_ge(x2_done, B * ET + 1)
        sp.wait_ge(R.w_first, 16)

    @block.tensor
    def _(pe):
        pe.sem_inc(acc_done, PRIME)
        pe.sem_inc(turned_done, PRIME)
        pe.sem_inc(inproj_done, PRIME)
        pe.wait_ge(yz_cleared, 1)
        keep_warm(pe, WARM_START, proj[:, 0, :], yz[:, 0:P], yz[:])
        pe.wait_ge(inT_in, 16)

        def input_projection(b, t, first=False):
            pe.wait_ge(ctx_in, (b + 1) * 16)
            if t > 1 and not first:
                if t - 2 in SUMMED:
                    pe.wait_ge(tap_done, b * ET + t - 1)
                else:
                    pe.wait_ge(conv_done, ET + (b - 1) * len(TAPPED) + TAPPED.index(t - 2) + 1)
            for c in range(KC):
                mm = pe.matmul(y_ps[:, t, :] if first else proj[:, t % 2, :], inT_sb[:, c, t * P:(t + 1) * P],
                               ctx_sb[:, c, :], start=c == 0, stop=c == KC - 1)
            mm.then_inc(inproj_done, 1)

        def conv_sum(b, p, t):
            pe.wait_ge(tap_done, b * ET + t + 1)
            if SUMMED.index(t):
                pe.wait_ge(conv_kept, (b - 1) * len(SUMMED) + SUMMED.index(t))
            for s in range(DC):
                source = delta[:, at(p), t, 0:L - s].rearrange("p o l -> p (o l)")
                mm = pe.matmul(conv_ps[:, s:], diag_w[:, t, s, :], source, start=s == 0, stop=s == DC - 1)
            mm.then_inc(conv_mm, 1)

        def x_projection(b, t):
            if t == 0:
                pe.wait_ge(u_done, b + 1)
            mm = pe.matmul(proj[0:DR + 2 * DS, 0, :], xprojT_sb[:, t, :], u[:, t, :],
                           start=t == 0, stop=t == ET - 1)
            if t == ET - 1:
                mm.then_inc(xd_mm, 1)

        def delta_projection(b, t, first=False):
            pe.wait_ge(xd_done, b + 1)
            if t > 1 and not first:
                pe.wait_ge(sp_read, b * ET + t - 1)
            pe.matmul(y_ps[:, t, :] if first else proj[:, t % 2, :], dtT_sb[:, t * P:(t + 1) * P], xd[0:DR, :],
                      start=True, stop=True).then_inc(delta_mm, 1)

        def turn(b, t):
            pe.wait_ge(gated, b * ET + t + 1 + PRIME)
            pe.wait_ge(x2_done, b * ET + t + 1)
            for l in range(LT):
                mm = pe.transpose(turned[:, l, :], yz[:, l * P:(l + 1) * P], ident)
            mm.then_inc(turned_done, 1)

        def turn_row(i):
            pe.wait_ge(R.rows_done, i + 1)
            if i > 1:
                pe.wait_ge(R.rowsT_done, i - 1)
            for c in range(HC):
                mm = pe.transpose(proj[:, i % 2, c * P:(c + 1) * P], row_buf[i][:, c * P:(c + 1) * P], ident)
            mm.then_inc(R.rows_turned, 1)

        def row_logits(i):
            if i == 0:
                pe.wait_ge(R.router_in, 32)
            pe.wait_ge(R.rowsT_done, i + 1)
            for c in range(HC):
                mm = pe.matmul(logits_ps[:, i, :], rowT_buf[i % KC][:, c * P:(c + 1) * P], R.gwT[:, c, :],
                               start=c == 0, stop=c == HC - 1)
            mm.then_inc(R.logits_mm, 1)

        def main(b, nb, np_):
            for k in range(UNITS):
                g, t, h, n = unit(k)
                if h == 0 and n == 0:
                    pe.wait_ge(gated, b * ET + t + 1 - ET + PRIME)
                    pe.matmul(y_ps[:, t, :], diag_d[:, t, :], u[:, t, :], start=True, stop=False)
                pe.wait_ge(hc_done, b * UNITS + k + 1 + PRIME)
                pe.matmul(y_ps[:, t, :], ident, states[:, k % RING, :], start=False,
                          stop=h == 1 and n == HALF - 1).then_inc(acc_done, 1)
                if g > ET and n == 5:
                    turn(b, t - 1)
                if nb is not None:
                    if k in IN_PROJ:
                        input_projection(nb, IN_PROJ.index(k))
                    if k in CONV and CONV.index(k) in SUMMED:
                        conv_sum(nb, np_, CONV.index(k))
                    if k in X_PROJ:
                        x_projection(nb, X_PROJ.index(k))
                    if k in DELTA_PROJ:
                        delta_projection(nb, DELTA_PROJ.index(k))
                else:
                    if k in TURN:
                        turn_row(TURN.index(k))
                    if k in LOGIT:
                        row_logits(LOGIT.index(k))
                    if k == RANK_SUMS:
                        rank_sums(pe, R, early, 0, rank_ps, count_ps)
            turn(b, ET - 1)

        for t in range(ET):
            input_projection(0, t, first=True)
        keep_warm(pe, WARM_CONV, proj[:, 0, :], yz[:, 0:P], yz[:])
        pe.wait_ge(consts_in, 16 * 5)
        for t in range(ET):
            x_projection(0, t)
        for t in range(ET):
            delta_projection(0, t, first=True)
        keep_warm(pe, WARM_MAIN, proj[:, 1, :], yz[:, 0:P], yz[:])
        pe.wait_ge(consts_made, 1)
        pe.wait_ge(sp_read, ET)
        pe.wait_ge(relu_done, ET)
        with pe.Fori(0, B - 1) as b:
            main(b, b + 1, (b + 1) % 2)
        main(B - 1, None, None)
        keep_warm(pe, WARM_ROUTER, proj[:, 0, :], ident, x2_all[:, 0, :])
        for q in range(late.n):
            pe.wait_ge(R.rows_done, late.lo + q + 1)
            for c in range(HC):
                mm = pe.transpose(y_ps[:, q, c * P:(c + 1) * P], late_row[:, q, c * P:(c + 1) * P], ident)
            mm.then_inc(R.rows_turned, 1)
        for q in range(late.n):
            pe.wait_ge(R.rowsT_done, late.lo + q + 1)
            for c in range(HC):
                mm = pe.matmul(late_logits_ps[:, q, :], late_rowT[:, q, c * P:(c + 1) * P], R.gwT[:, c, :],
                               start=c == 0, stop=c == HC - 1)
            mm.then_inc(R.logits_mm, 1)
        rank_sums(pe, R, late, 1, late_rank_ps, late_count_ps)

    @block.scalar
    def _(act):
        act.wait_ge(consts_in, 16 * 5)
        act.activation(gate[:], gate[:], ACT.Tanh).then_inc(a_exp, 1)
        act.activation(a_neg, a_neg, ACT.Exp).then_inc(a_exp, 1)

        def first_tap(b, p, t, first=False):
            act.wait_ge(inproj_done, b * ET + t + 1 + PRIME)
            source = y_ps[:, t, :] if first else proj[:, t % 2, :]
            if t in SUMMED and not first:
                act.activation(delta[:, at(p), t, :], source, ACT.Copy).then_inc(tap_done, 1)
            else:
                act.activation(delta[:, at(p), t, :], source, ACT.Identity, scale=chan_sb[:, t, CW + DC - 1:CW + DC],
                               bias=chan_sb[:, t, CB:CB + 1]).then_inc(tap_done, 1)

        def keep_conv(b, p, t):
            act.wait_ge(conv_mm, summed)
            act.reg_add(summed, summed, 1)
            act.activation(delta[:, at(p), t, :], conv_ps[:], ACT.Identity, bias=chan_sb[:, t, CB:CB + 1])\
               .then_inc(conv_kept, 1)

        def silu_u(b, p, first=False):
            if not first:
                act.wait_ge(acc_done, u_summed)
                act.reg_add(u_summed, u_summed, UNITS)
                act.wait_ge(du_done, b * ET)
                if SUMMED:
                    act.wait_ge(conv_kept, kept)
                    act.reg_add(kept, kept, len(SUMMED))
                act.wait_ge(conv_done, convolved)
                act.reg_add(convolved, convolved, len(TAPPED))
            else:
                act.wait_ge(conv_done, ET)
            act.activation(u[:], delta[:, at(p), :, :], ACT.Silu).then_inc(u_done, 1)

        def silu_z(b):
            act.wait_ge(ln_done, b + 1)
            act.wait_ge(gated, b * ET + PRIME)
            for t in range(ET):
                act.activation(sz[:, t, :], x2_all[:, at(b * LT + t), :], ACT.Silu,
                               scale=rstd[:, t:t + 1], bias=neg_mr[:, t:t + 1]).then_inc(sz_done, 1)

        def keep_xd(b, first=False):
            act.wait_ge(xd_mm, b + 1)
            if not first:
                act.wait_ge(xs_out, b * 16)
            act.activation(xd[:], proj[0:DR + 2 * DS, 0, :], ACT.Copy).then_inc(xd_done, 1)

        def softplus(b, p, t, first=False):
            v = y_ps[:, t, :] if first else proj[:, t % 2, :]
            act.wait_ge(delta_mm, b * ET + t + 1)
            if not first:
                act.activation(du[:, at(p), t, :], v, ACT.Relu, bias=chan_sb[:, t, CDT:CDT + 1])
            act.activation(delta[:, at(p), t, :], v, ACT.Abs, bias=chan_sb[:, t, CDT:CDT + 1]).then_inc(sp_read, 1)

        def softplus_exp(b, p):
            act.wait_ge(sp_read, sp_step)
            act.reg_add(sp_step, sp_step, ET)
            act.activation(delta[:, at(p), :, :], delta[:, at(p), :, :], ACT.Exp, scale=-1.0).then_inc(sp_exp, 1)

        def softplus_ln(b, p):
            act.wait_ge(sp_exp, ln_step)
            act.reg_add(ln_step, ln_step, 1)
            act.activation(delta[:, at(p), :, :], delta[:, at(p), :, :], ACT.Ln, bias=1.0).then_inc(sp_ln, 1)

        def normalise(i):
            if i == 0:
                act.wait_ge(R.nmr_done, 1)
                act.wait_ge(ys_cleared, 16)
                act.wait_ge(gated, (B - 1) * ET + PRIME)
            act.activation(row_buf[i], x2_all[:, i, :], ACT.Identity, scale=R.rs[:, i:i + 1], bias=R.nmr[:, i:i + 1])\
               .then_inc(R.rows_done, 1)

        def keep_turned(i):
            act.wait_ge(R.rows_turned, i + 1)
            if i >= KC:
                act.wait_ge(R.logits_mm, i - KC + 1)
            act.activation(rowT_buf[i % KC], proj[:, i % 2, :], ACT.Copy).then_inc(R.rowsT_done, 1)

        def main(b, p, nb, np_):
            for k in range(UNITS):
                g, t, h, n = unit(k)
                if h == 0 and n == 0:
                    act.wait_ge(delta_done, b * ET + t + 1)
                act.wait_ge(acc_done, ring_free)
                act.reg_add(ring_free, ring_free, 1)
                act.activation(states[:, k % RING, :], delta[:, at(p), t, :], ACT.Exp,
                               scale=a_neg[:, t, h * HALF + n:h * HALF + n + 1]).then_inc(decay_done, 1)
                if k == GATE_SILU:
                    silu_z(b)
                if nb is not None:
                    if k in TAP:
                        first_tap(nb, np_, TAP.index(k))
                    if k in KEEP_CONV:
                        keep_conv(nb, np_, SUMMED[KEEP_CONV.index(k)])
                    if k == U_SILU:
                        silu_u(nb, np_)
                    if k == KEEP_XD:
                        keep_xd(nb)
                    if k in SOFTPLUS:
                        softplus(nb, np_, SOFTPLUS.index(k))
                    if k == SOFTPLUS_EXP:
                        softplus_exp(nb, np_)
                        softplus_ln(nb, np_)
                else:
                    if k in ROW:
                        normalise(ROW.index(k))
                    if k in KEEP_TURNED:
                        keep_turned(KEEP_TURNED.index(k))

        convolved = act.alloc_register("convolved")
        act.reg_mov(convolved, ET + len(TAPPED))
        kept = act.alloc_register("kept")
        act.reg_mov(kept, len(SUMMED))
        summed = act.alloc_register("summed")
        act.reg_mov(summed, 1)
        for t in range(ET):
            first_tap(0, 0, t, first=True)
        silu_u(0, 0, first=True)
        keep_xd(0, first=True)
        sp_step = act.alloc_register("sp_step")
        ln_step = act.alloc_register("ln_step")
        act.reg_mov(sp_step, ET)
        act.reg_mov(ln_step, 1)
        for t in range(ET):
            softplus(0, 0, t, first=True)
        softplus_exp(0, 0)
        softplus_ln(0, 0)
        act.wait_ge(signs_made, 1)
        ring_free = act.alloc_register("ring_free")
        u_summed = act.alloc_register("u_summed")
        act.reg_mov(ring_free, PRIME + 1 - RING)
        act.reg_mov(u_summed, PRIME + HALF * (ET - 1) + 1)
        with act.Fori(0, B - 1) as b:
            main(b, b % 2, b + 1, (b + 1) % 2)
        main(B - 1, (B - 1) % 2, None, None)
        act.wait_ge(R.nmr_done, 2)
        for q in range(late.n):
            t = late.lo + q
            act.activation(late_row[:, q, :], x2_all[:, t, :], ACT.Identity,
                           scale=R.rs[:, t:t + 1], bias=R.nmr[:, t:t + 1]).then_inc(R.rows_done, 1)

    @block.gpsimd
    def _(pool):
        pool.memset(half_pow[:], -0.5).then_inc(pows_made, 1)

        def inverse_root(b):
            pool.wait_ge(sz_done, b * ET + PRIME)
            pool.wait_ge(aggr_done, rows_ready)
            pool.reg_add(rows_ready, rows_ready, ET)
            pool.tensor_scalar(rstd[:], mean_var[:, :, 1], EPS, 1.0, ALU.add, ALU.mult).then_inc(var_eps, 1)
            pool.wait_ge(var_eps, b + 1)
            pool.tensor_tensor(rstd[:], rstd[:], half_pow[:], ALU.pow).then_inc(rstd_done, 1)

        def times_u(b, p, t):
            pool.wait_ge(delta_done, deltas)
            pool.reg_add(deltas, deltas, 1)
            pool.tensor_tensor(du[:, at(p), t, :], delta[:, at(p), t, :], u[:, t, :], ALU.mult).then_inc(du_done, 1)

        def main(b, p, nb, np_):
            for j in range(UNITS // 2):
                g, t, h, n = unit(2 * j)
                if h == 0 and n == 0:
                    pool.wait_ge(du_done, du_step)
                    pool.reg_add(du_step, du_step, 1)
                if t == 0 and n == 0:
                    pool.wait_ge(bc_in[h][0], b * 16 + 16)
                pool.wait_ge(scan_done, buffer_free)
                pool.reg_add(buffer_free, buffer_free, 2)
                pool.tensor_tensor(dbu[:, j % PAIR_RING, :, :], du[:, at(p), t, :].to_broadcast([P, 2, L]),
                                   bc[:, h, 0, n:n + 2, :], ALU.mult).then_inc(dbu_done, 1)
                if g < ET - 1 and n == 2:
                    times_u(b, p, t + 1)
                if nb is not None and 2 * j == STATS_ROOT:
                    inverse_root(nb)
                if nb is not None and 2 * j == DELTA[0] + 4:
                    times_u(nb, np_, 0)
                if nb is None and 2 * j == ROOT:
                    row_roots(pool, R, early, 0)

        pool.memset(zeros, 0.0).then_inc(zeros_made, 1)
        pool.memset(R.neg_half[:], -0.5).then_inc(pows_made, 1)
        pool.sem_inc(sz_done, PRIME)
        pool.wait_ge(pows_made, 2)
        rows_ready = pool.alloc_register("rows_ready")
        buffer_free = pool.alloc_register("buffer_free")
        pool.reg_mov(rows_ready, ET)
        du_step = pool.alloc_register("du_step")
        deltas = pool.alloc_register("deltas")
        pool.reg_mov(buffer_free, PRIME + 2 - 2 * PAIR_RING)
        pool.reg_mov(du_step, 1)
        pool.reg_mov(deltas, 1)
        inverse_root(0)
        times_u(0, 0, 0)
        with pool.Fori(0, B - 1) as b:
            main(b, b % 2, b + 1, (b + 1) % 2)
        main(B - 1, (B - 1) % 2, None, None)
        pool.wait_ge(R.pos_done, 1)
        for i in range(EARLY):
            if i == ROOT_LATE:
                row_roots(pool, R, late, 1)
            scatter_rows(pool, R, i, row_buf[i], xs_dram)
        pool.wait_ge(R.scattered, 16 * TOP * EARLY)

    @block.vector
    def _(dve):
        dve.memset(yz[:], 0.0).then_inc(yz_cleared, 1)
        dve.sem_inc(scan_done, PRIME)
        dve.sem_inc(hc_done, PRIME)
        dve.sem_inc(gated, PRIME)
        dve.sem_inc(x2_done, 1)
        dve.wait_ge(consts_in, 16 * 5)
        dve.wait_ge(a_exp, 2)
        dve.tensor_scalar(a_neg, a_neg, -1.0, None, ALU.mult).then_inc(signs_made, 1)

        def row_stats(b, t):
            if t == 0:
                dve.wait_ge(x_in, (b + 1) * 16)
            dve.bn_stats(stats[:, t, :], x2_all[:, at(b * LT + t), :]).then_inc(stats_done, 1)

        def row_aggr(b):
            dve.wait_ge(stats_done, rows_seen)
            dve.reg_add(rows_seen, rows_seen, ET)
            for t in range(ET):
                dve.bn_aggr(mean_var[:, t, :], stats[:, t, :]).then_inc(aggr_done, 1)

        def row_shift(b):
            dve.wait_ge(rstd_done, b + 1)
            dve.scalar_tensor_tensor(out=neg_mr[:], in0=mean_var[:, :, 0], scalar=-1.0, in1=rstd[:],
                                     op0=ALU.mult, op1=ALU.mult).then_inc(ln_done, 1)

        def other_taps(b, p, t, first=False):
            source = y_ps[:, t, :] if first else proj[:, t % 2, :]
            step_no = 2 * t if first else 2 * (ET + (b - 1) * len(TAPPED) + TAPPED.index(t))
            dve.wait_ge(tap_done, b * ET + t + 1)
            for s in range(1, DC):
                if s > 1:
                    dve.wait_ge(conv_step, step_no + s - 1)
                acc = delta[:, at(p), t, s:]
                dve.scalar_tensor_tensor(out=acc, in0=source[:, 0:L - s], scalar=chan_sb[:, t, CW + DC - 1 - s:CW + DC - s],
                                         in1=acc, op0=ALU.mult, op1=ALU.add)\
                   .then_inc(conv_step if s < DC - 1 else conv_done, 1)

        def first_relu(t):
            dve.wait_ge(sp_read, t + 1)
            dve.tensor_scalar(du[:, 0, t, :], y_ps[:, t, :], chan_sb[:, t, CDT:CDT + 1], 0.0, ALU.add, ALU.max)\
               .then_inc(relu_done, 1)

        def add_delta(b, p, t):
            dve.wait_ge(sp_ln, b + 1)
            dve.tensor_tensor(delta[:, at(p), t, :], delta[:, at(p), t, :], du[:, at(p), t, :], ALU.add)\
               .then_inc(delta_done, 1)

        def times_c(b, k):
            g, t, h, n = unit(k)
            if t == 0 and n == 0:
                dve.wait_ge(bc_in[h][1], b * 16 + 16)
            dve.wait_ge(scan_done, b * UNITS + k + 1 + PRIME)
            product = states[:, k % RING, :]
            dve.tensor_tensor(product, product, bc[:, h, 1, n, :], ALU.mult).then_inc(hc_done, 1)

        def gate_y(b, p, t):
            g = ET + t
            dve.wait_ge(turned_done, b * ET + t + PRIME)
            if t == 0:
                dve.wait_ge(sz_done, b * ET + ET + PRIME)
            dve.wait_ge(acc_done, b * UNITS + HALF * (g + 1) + PRIME)
            dve.tensor_tensor(yz[:], y_ps[:, t, :], sz[:, t, :], ALU.mult).then_inc(gated, 1)

        def residual(b, t):
            dve.wait_ge(turned_done, b * ET + t + 1 + PRIME)
            cols = x2_all[:, at(b * LT, LT), t * P:(t + 1) * P]
            dve.scalar_tensor_tensor(out=cols, in0=turned[:], scalar=gate[:, 0:1], in1=cols,
                                     op0=ALU.mult, op1=ALU.add).then_inc(x2_done, 1)

        def main(b, p, nb, np_):
            for k in range(UNITS):
                g, t, h, n = unit(k)
                dve.wait_ge(decay_done, b * UNITS + k + 1)
                if n % 2 == 0:
                    dve.wait_ge(dbu_done, b * (UNITS // 2) + k // 2 + 1)
                state = states[:, k % RING, :]
                dve.tensor_tensor_scan(state, state, dbu[:, k // 2 % PAIR_RING, k % 2, :], 0.0,
                                       ALU.mult, ALU.add).then_inc(scan_done, 1)
                if k:
                    times_c(b, k - 1)
                if g > ET and n == 3:
                    gate_y(b, p, t - 1)
                if g > ET and n == 7:
                    residual(b, t - 1)
                if nb is not None:
                    if STATS <= k < STATS + ET:
                        row_stats(nb, k - STATS)
                    if k == STATS_AGGR:
                        row_aggr(nb)
                    if k == STATS_SHIFT:
                        row_shift(nb)
                    if k in CONV and CONV.index(k) in TAPPED:
                        other_taps(nb, np_, CONV.index(k))
                    if k in DELTA:
                        add_delta(nb, np_, DELTA.index(k))
                else:
                    if k == 0:
                        dve.wait_ge(x2_done, b * ET + 1)
                    if k < EARLY // TILES_A_UNIT:
                        for i in range(k * TILES_A_UNIT, (k + 1) * TILES_A_UNIT):
                            dve.bn_stats(R.st[:, i, :], x2_all[:, i, :]).then_inc(R.st_done, 1)
                    if k == AGGR:
                        dve.wait_ge(R.st_done, EARLY)
                        for i in range(EARLY):
                            dve.bn_aggr(R.mv[:, i, :], R.st[:, i, :]).then_inc(R.mv_done, 1)
                    if k == SHIFT:
                        row_shifts(dve, R, early, 0)
                    if k in CHOOSE:
                        choose(dve, R, early, CHOOSE.index(k), logits_ps)
                    if k == RANKS:
                        places(dve, R, early, 0, rank_ps, count_ps)
            times_c(b, UNITS - 1)
            gate_y(b, p, ET - 1)
            residual(b, ET - 1)

        rows_seen = dve.alloc_register("rows_seen")
        dve.reg_mov(rows_seen, ET)
        for t in range(ET):
            other_taps(0, 0, t, first=True)
        for t in range(ET):
            row_stats(0, t)
        row_aggr(0)
        row_shift(0)
        for t in range(ET):
            for s in range(DC) if t in SUMMED else ():
                dve.tensor_scalar(diag_w[:, t, s, :], ident, chan_sb[:, t, CW + DC - 1 - s:CW + DC - s], None, ALU.mult)
            mk = dve.tensor_scalar(diag_d[:, t, :], ident, chan_sb[:, t, CD:CD + 1], None, ALU.mult)
        mk.then_inc(consts_made, 1)
        for t in range(ET):
            first_relu(t)
        dve.wait_ge(relu_done, ET)
        for t in range(ET):
            add_delta(0, 0, t)
        with dve.Fori(0, B - 1) as b:
            main(b, b % 2, b + 1, (b + 1) % 2)
        main(B - 1, (B - 1) % 2, None, None)
        dve.wait_ge(x2_done, B * ET + 1)
        for i in range(late.lo, late.hi):
            dve.bn_stats(R.st[:, i, :], x2_all[:, i, :]).then_inc(R.st_done, 1)
        dve.wait_ge(R.st_done, NT)
        for i in range(late.lo, late.hi):
            dve.bn_aggr(R.mv[:, i, :], R.st[:, i, :]).then_inc(R.mv_done, 1)
        row_shifts(dve, R, late, 1)
        for q in range(late.n):
            dve.wait_ge(R.rows_turned, late.lo + q + 1)
            dve.tensor_copy(late_rowT[:, q, :], y_ps[:, q, :]).then_inc(R.rowsT_done, 1)
        choose(dve, R, late, 0, late_logits_ps)
        choose(dve, R, late, 1, late_logits_ps)
        places(dve, R, late, 1, late_rank_ps, late_count_ps)


def moe_block(nc, ctx, R, shared, x2_all, out, w_all, b_all, g_ffn, xs_dram, ys_dram):

    def sb(name, shape, dt=F32):
        return ctx.enter_context(nc.sbuf_tensor(name, shape, dt))

    def sem(name):
        return ctx.enter_context(nc.semaphore(name))

    def at(i, n=1):
        return bass.ds(i, n)

    late = R.groups[1]
    ident = R.ident
    gate2 = sb("gate2", [P, 1])
    prob = sb("prob", [P, 2, NT])
    total = sb("total", [P, E])
    pad_f = sb("pad_f", [P, E])
    pad_row = sb("pad_row", [P, E], I32)
    blocks_f = sb("blocks_f", [P, E])
    blocks_i = sb("blocks_i", [P, E], I32)
    ends_f = sb("ends_f", [P, E])
    ends_i = sb("ends_i", [P, E], I32)
    base = sb("base", [P, E])
    slot_expert = sb("slot_expert", [P, SLOTS], I32)
    skipped = sb("skipped", [P, E])
    slot_row = sb("slot_row", [P, SLOTS], I32)
    shift = sb("shift", [P, E])
    pos_y_f = sb("pos_y_f", [P, 2, NT])
    pos_y = sb("pos_y", [P, 2, NT], U32)
    lower = sb("lower", [P, 2, NT])
    weight = sb("weight", [P, 2, NT])
    part = sb("part", [P, 2, NT])

    sizes = (WCOLS, 4 * H, 4 * I, 2 * BCOLS, H, SLOTS * E, SLOTS * E, SLOTS, SLOTS, SLOTS, EARLY * E, (NT - EARLY) * E, 2 * H)
    ends = np.cumsum(sizes)
    stage, rows, inner, bias, yo, past, skips, slot_f, used_slot, slot_skip, shift0, shift1, spare = (
        shared[:, e - n:e] for e, n in zip(ends.tolist(), sizes))
    rows = rows.rearrange("p (q h) -> p q h", q=4)
    inner = inner.rearrange("p (q i) -> p q i", q=4)
    glu, sig, lin, act_y = (inner[:, q, :] for q in range(4))
    bias = bias.rearrange("p (e n) -> p e n", e=2)
    low_row = [stage[:, i * H:(i + 1) * H] for i in range(WCOLS // H)] + [rows[:, q, :] for q in (2, 3)]
    low_row += [spare[:, i * H:(i + 1) * H] for i in range(NT - len(low_row))]
    free_row = [inner[:, q, :] for q in range(4)] + [rows[:, q, :] for q in (0, 1)]
    high_row = free_row + low_row[:NT - len(free_row)]
    past, skips, *shifts = (a.rearrange("p (n e) -> p n e", e=E) for a in (past, skips, shift0, shift1))
    xT_hi, xT_lo = (sb(name, [P, HC, P], F32R) for name in ("xT_hi", "xT_lo"))
    yT_hi, yT_lo = (sb(name, [P, IC, P], F32R) for name in ("yT_hi", "yT_lo"))
    w_hi = sb("w_hi", [P, 2, WCOLS], F32R)
    w_lo = sb("w_lo", [P, 2, WCOLS], F32R)

    banks = ctx.enter_context(nc.psum_tensor("banks", [P, 4, 512], F32))
    xT_ps, yT_ps, glu_ps, lin_ps = (banks[:, q, :] for q in range(4))
    out_ps = ctx.enter_context(nc.psum_tensor("out_ps", [P, H], F32))
    gate2_in = sem("gate2_in")
    gate2_done = sem("gate2_done")
    diff_done = sem("diff_done")
    exp_done = sem("exp_done")
    slots_known = sem("slots_known")
    zeros_made = sem("zeros_made")
    pads_out = sem("pads_out")
    w_in = sem("w_in")
    bias_in = sem("bias_in")
    hi_done = sem("hi_done")
    split_done = sem("split_done")
    xg_in = [sem(f"xg_in{q}") for q in range(2)]
    xT_mm = sem("xT_mm")
    xT_hi_done = sem("xT_hi_done")
    xT_lo_done = sem("xT_lo_done")
    glu_mm = sem("glu_mm")
    lin_mm = sem("lin_mm")
    glu_done = sem("glu_done")
    sig_done = sem("sig_done")
    lin_done = sem("lin_done")
    gs_done = sem("gs_done")
    act_done = sem("act_done")
    yT_mm = sem("yT_mm")
    yT_hi_done = sem("yT_hi_done")
    yT_lo_done = sem("yT_lo_done")
    out_mm = sem("out_mm")
    yo_done = sem("yo_done")
    ys_out = sem("ys_out")
    places_known = sem("places_known")
    low_rows_out = sem("low_rows_out")
    low_rows_in = sem("low_rows_in")
    high_row_in = [sem(f"high_row_in{i}") for i in range(NT)]
    low_added = sem("low_added")
    high_added = sem("high_added")
    out_out = sem("out_out")

    def store_pads(eng, half):
        with eng.Fori(half * E // 2, (half + 1) * E // 2) as e:
            row = eng.value_load(pad_row[0:1, at(e)], min_val=0, max_val=E * REGION - P)
            eng.dma_start(xs_dram[at(row, P), :], yo).then_inc(pads_out, 16)

    block = ctx.enter_context(nc.Block())

    @block.sync
    def _(sp):
        sp.dma_start(gate2[:], g_ffn.to_broadcast([P, 1])).then_inc(gate2_in, 16)
        sp.sem_inc(ys_out, 16)
        sp.wait_ge(zeros_made, 1)
        sp.wait_ge(slots_known, 1)
        store_pads(sp, 0)
        first_row = [sp.value_load(slot_row[0:1, q:q + 1], min_val=0, max_val=E * REGION - P) for q in range(2)]
        sp.wait_ge(pads_out, 16 * E)
        sp.wait_ge(R.scattered, 16 * TOP * NT)

        def load_rows(s, q):
            row = sp.value_load(slot_row[0:1, at(s)], min_val=0, max_val=E * REGION - P)
            sp.dma_start(rows[:, q, :], xs_dram[at(row, P), :]).then_inc(xg_in[q], 16)

        def load_slot(s, q):
            sp.wait_ge(xT_mm, s - 1)
            load_rows(s, q)

        def store_slot(s):
            sp.wait_ge(yo_done, s + 1 + PRIME)
            sp.dma_start(ys_dram[at(s * P, P), :], yo).then_inc(ys_out, 16)

        for q in range(2):
            sp.dma_start(rows[:, q, :], xs_dram[at(first_row[q], P), :]).then_inc(xg_in[q], 16)
        load_slot(2, 0)
        with sp.Fori(0, PAIRS) as j:
            for q in range(2):
                s = j * 2 + q + 1
                load_slot(s + 2, 1 - q)
                store_slot(s - 1)
        for s in range(2 * PAIRS, SLOTS):
            store_slot(s)
        with sp.Fori(0, NT) as i:
            sp.wait_ge(high_added, i + 1)
            sp.dma_start(out[at(i * P, P), :], x2_all[:, at(i), :].rearrange("p o d -> p (o d)")).then_inc(out_out, 16)
        sp.wait_ge(out_out, 16 * NT)

    @block.tensor
    def _(pe):
        pe.wait_ge(slots_known, 1)
        keep_warm(pe, WARM_SLOTS, out_ps[:], ident, x2_all[:, 0, :])

        def turn_x(s, q):
            pe.wait_ge(xg_in[q], (s - q) * 8 + 16)
            pe.wait_ge(xT_lo_done, s + PRIME)
            for c in range(HC):
                mm = pe.transpose(xT_ps[:, c * P:(c + 1) * P], rows[:, q, c * P:(c + 1) * P], ident)
            mm.then_inc(xT_mm, 1)

        def turn_y(s):
            pe.wait_ge(act_done, s + 1)
            pe.wait_ge(yT_lo_done, s + PRIME)
            for c in range(IC):
                mm = pe.transpose(yT_ps[:, c * P:(c + 1) * P], act_y[:, c * P:(c + 1) * P], ident)
            mm.then_inc(yT_mm, 1)

        def product(acc, hi, lo, chunks, par, col, width, done):
            for c in range(chunks):
                for n, (a, w) in enumerate(((hi, w_hi), (hi, w_lo), (lo, w_hi))):
                    cols = w[:, at(par), col + c * width:col + c * width + 512]
                    mm = pe.matmul(acc, a[:, c, :], cols.rearrange("p o n -> p (o n)"),
                                   start=c == 0 and n == 0, stop=c == chunks - 1 and n == 2)
            mm.then_inc(done, 1)

        def up(s, e, half):
            if half == 0:
                pe.wait_ge(split_done, e + 1)
                pe.wait_ge(xT_lo_done, s + 1 + PRIME)
                pe.wait_ge(glu_done, s + PRIME)
                product(glu_ps, xT_hi, xT_lo, HC, e % 2, 0, 2 * I, glu_mm)
            else:
                pe.wait_ge(lin_done, s + PRIME)
                product(lin_ps, xT_hi, xT_lo, HC, e % 2, I, 2 * I, lin_mm)

        def down(s, par):
            pe.wait_ge(yT_lo_done, s + 1 + PRIME)
            pe.wait_ge(yo_done, s + PRIME)
            product(out_ps[:], yT_hi, yT_lo, IC, par, HC * 2 * I, H, out_mm)

        def slot(s, q):
            e = pe.value_load(slot_expert[0:1, at(s)], min_val=0, max_val=E - 1)
            e_last = pe.value_load(slot_expert[0:1, at(s - 1)], min_val=0, max_val=E - 1)
            up(s, e, 0)
            turn_y(s - 1)
            up(s, e, 1)
            turn_x(s + 1, 1 - q)
            down(s - 1, e_last % 2)

        turn_x(0, 0)
        up(0, 0, 0)
        up(0, 0, 1)
        turn_x(1, 1)
        with pe.Fori(0, PAIRS) as j:
            for q in range(2):
                slot(j * 2 + q + 1, 1 - q)
        slot(SLOTS - 2, (SLOTS - 2) % 2)
        e = pe.value_load(slot_expert[0:1, SLOTS - 1:SLOTS], min_val=0, max_val=E - 1)
        e_last = pe.value_load(slot_expert[0:1, SLOTS - 2:SLOTS - 1], min_val=0, max_val=E - 1)
        up(SLOTS - 1, e, 0)
        turn_y(SLOTS - 2)
        up(SLOTS - 1, e, 1)
        down(SLOTS - 2, e_last % 2)
        turn_y(SLOTS - 1)
        down(SLOTS - 1, e % 2)

    @block.scalar
    def _(act):
        act.wait_ge(gate2_in, 16)
        act.activation(gate2[:], gate2[:], ACT.Tanh).then_inc(gate2_done, 1)
        act.wait_ge(R.w_first, 16)
        act.activation(w_hi[:, 0, :], stage, ACT.Copy).then_inc(hi_done, 1)
        act.wait_ge(zeros_made, 1)
        act.wait_ge(slots_known, 1)
        store_pads(act, 1)
        act.wait_ge(diff_done, 1)
        act.activation(prob[:, 1, :], prob[:, 1, :], ACT.Exp).then_inc(exp_done, 1)

        def keep_xT(s):
            act.wait_ge(xT_mm, s + 1)
            act.activation(xT_hi[:].rearrange("p c t -> p (c t)"), xT_ps, ACT.Copy).then_inc(xT_hi_done, 1)

        def sigmoid(s):
            act.wait_ge(glu_done, s + 1 + PRIME)
            act.activation(sig, glu, ACT.Sigmoid, scale=1.702).then_inc(sig_done, 1)

        def keep_yT(s):
            act.wait_ge(yT_mm, s + 1)
            act.activation(yT_hi[:].rearrange("p c t -> p (c t)"), yT_ps, ACT.Copy).then_inc(yT_hi_done, 1)

        keep_xT(0)
        sigmoid(0)
        keep_xT(1)
        with act.Fori(1, SLOTS - 1) as s:
            sigmoid(s)
            keep_yT(s - 1)
            keep_xT(s + 1)
        sigmoid(SLOTS - 1)
        keep_yT(SLOTS - 2)
        keep_yT(SLOTS - 1)

    @block.vector
    def _(dve):
        dve.sem_inc(xT_lo_done, PRIME)
        dve.sem_inc(yT_lo_done, PRIME)
        dve.sem_inc(glu_done, PRIME)
        dve.sem_inc(lin_done, PRIME)
        dve.sem_inc(yo_done, PRIME)
        dve.wait_ge(zeros_made, 1)
        step(dve, R, dve.tensor_copy(total[:], late.count[:, :, late.n - 1]))
        step(dve, R, dve.tensor_tensor(pad_f[:], total[:], R.region, ALU.add))
        dve.tensor_copy(pad_row[:], pad_f[:])
        step(dve, R, dve.tensor_scalar(blocks_f[:], total[:], 1.0, float(P - 1), ALU.max, ALU.add))
        step(dve, R, dve.tensor_copy(blocks_i[:], blocks_f[:]))
        step(dve, R, dve.tensor_scalar(blocks_i[:], blocks_i[:], 7, None, ALU.arith_shift_right))
        step(dve, R, dve.tensor_copy(blocks_f[:], blocks_i[:]))
        step(dve, R, dve.tensor_tensor_scan(ends_f[:], R.ones[:, 0:E], blocks_f[:], 0.0, ALU.mult, ALU.add))
        dve.tensor_copy(ends_i[:], ends_f[:])
        step(dve, R, dve.tensor_scalar(base[:], ends_f[:], 1.0, None, ALU.subtract))
        step(dve, R, dve.tensor_scalar(used_slot, R.slot_no, base[:, E - 1:E], None, ALU.min))
        step(dve, R, dve.tensor_tensor(past, used_slot.unsqueeze(2).to_broadcast([P, SLOTS, E]),
                                       ends_f[:].unsqueeze(1).to_broadcast([P, SLOTS, E]), ALU.is_ge))
        step(dve, R, dve.tensor_reduce(slot_f, past, AX.X, ALU.add))
        dve.tensor_copy(slot_expert[:], slot_f)
        step(dve, R, dve.tensor_scalar(skipped[:], blocks_f[:], -float(P), float(REGION), ALU.mult, ALU.add))
        step(dve, R, dve.tensor_tensor(skips, past, skipped[:].unsqueeze(1).to_broadcast([P, SLOTS, E]),
                                       ALU.mult))
        step(dve, R, dve.tensor_reduce(slot_skip, skips, AX.X, ALU.add))
        step(dve, R, dve.scalar_tensor_tensor(out=slot_f, in0=used_slot, scalar=float(P), in1=slot_skip,
                                              op0=ALU.mult, op1=ALU.add))
        dve.tensor_copy(slot_row[:], slot_f).then_inc(slots_known, 1)
        dve.wait_ge(hi_done, 1)
        dve.tensor_tensor(w_lo[:, 0, :], stage, w_hi[:, 0, :].bitcast(F32), ALU.subtract).then_inc(split_done, 1)
        dve.tensor_tensor(prob[:, 1, :], R.top[:, 1, :], R.top[:, 0, :], ALU.subtract).then_inc(diff_done, 1)
        step(dve, R, dve.tensor_tensor(shift[:], ends_f[:], blocks_f[:], ALU.subtract))
        step(dve, R, dve.scalar_tensor_tensor(out=shift[:], in0=shift[:], scalar=float(P), in1=R.region,
                                              op0=ALU.mult, op1=ALU.subtract))
        for g, G in enumerate(R.groups):
            for r in range(2):
                step(dve, R, dve.tensor_tensor(shifts[g], G.onehot[r][:],
                                               shift[:].unsqueeze(1).to_broadcast([P, G.n, E]), ALU.mult))
                step(dve, R, dve.tensor_reduce(pos_y_f[:, r, G.lo:G.hi], shifts[g], AX.X, ALU.add))
        step(dve, R, dve.tensor_tensor(pos_y_f[:], pos_y_f[:], R.pos_f[:], ALU.add))
        for r in range(2):
            step(dve, R, dve.tensor_tensor(lower[:, r, :], pos_y_f[:, r, :], pos_y_f[:, 1 - r, :], ALU.is_lt))
        step(dve, R, dve.tensor_tensor(part[:, 0, :], pos_y_f[:, 0, :], pos_y_f[:, 1, :], ALU.min))
        step(dve, R, dve.tensor_tensor(part[:, 1, :], pos_y_f[:, 0, :], pos_y_f[:, 1, :], ALU.max))
        step(dve, R, dve.tensor_copy(pos_y[:], part[:]))
        dve.wait_ge(exp_done, 1)
        step(dve, R, dve.tensor_scalar(part[:, 0, :], prob[:, 1, :], 1.0, None, ALU.add))
        step(dve, R, dve.reciprocal(prob[:, 0, :], part[:, 0, :]))
        dve.wait_ge(gate2_done, 1)
        step(dve, R, dve.tensor_scalar(prob[:, 0, :], prob[:, 0, :], gate2[:, 0:1], None, ALU.mult))
        step(dve, R, dve.tensor_tensor(prob[:, 1, :], prob[:, 1, :], prob[:, 0, :], ALU.mult))
        for r in range(2):
            step(dve, R, dve.tensor_tensor(weight[:, r, :], prob[:, 0, :], lower[:, r, :], ALU.mult))
            step(dve, R, dve.tensor_tensor(part[:, r, :], prob[:, 1, :], lower[:, 1 - r, :], ALU.mult))
        dve.tensor_tensor(weight[:], weight[:], part[:], ALU.add).then_inc(places_known, 1)

        def rest_of_xT(s):
            dve.wait_ge(xT_hi_done, s + 1)
            dve.tensor_tensor(xT_lo[:].rearrange("p c t -> p (c t)"), xT_ps,
                              xT_hi[:].rearrange("p c t -> p (c t)").bitcast(F32), ALU.subtract).then_inc(xT_lo_done, 1)

        def glu_bias(s, par):
            dve.wait_ge(glu_mm, s + 1)
            dve.tensor_tensor(glu, glu_ps, bias[:, at(par), 0:I].rearrange("p o n -> p (o n)"), ALU.add)\
               .then_inc(glu_done, 1)

        def activate(s, par):
            dve.wait_ge(sig_done, s + 1)
            dve.tensor_tensor(sig, glu, sig, ALU.mult).then_inc(gs_done, 1)
            dve.wait_ge(lin_mm, s + 1)
            dve.scalar_tensor_tensor(out=lin, in0=lin_ps, scalar=1.0, op0=ALU.add, op1=ALU.add,
                                     in1=bias[:, at(par), I:2 * I].rearrange("p o n -> p (o n)"))\
               .then_inc(lin_done, 1)
            dve.wait_ge(gs_done, s + 1)
            dve.wait_ge(lin_done, s + 1 + PRIME)
            dve.tensor_tensor(act_y, sig, lin, ALU.mult).then_inc(act_done, 1)

        def rest_of_yT(s):
            dve.wait_ge(yT_hi_done, s + 1)
            dve.tensor_tensor(yT_lo[:].rearrange("p c t -> p (c t)"), yT_ps,
                              yT_hi[:].rearrange("p c t -> p (c t)").bitcast(F32), ALU.subtract).then_inc(yT_lo_done, 1)

        def keep_out(s, par):
            dve.wait_ge(out_mm, s + 1)
            dve.wait_ge(ys_out, s * 16 + 16)
            dve.tensor_tensor(yo, out_ps[:], bias[:, at(par), 2 * I:].rearrange("p o n -> p (o n)"), ALU.add)\
               .then_inc(yo_done, 1)

        dve.wait_ge(pads_out, 16 * E)
        rest_of_xT(0)
        dve.wait_ge(bias_in, 16)
        glu_bias(0, 0)
        rest_of_xT(1)
        activate(0, 0)
        with dve.Fori(1, SLOTS - 1) as s:
            e = dve.value_load(slot_expert[0:1, at(s)], min_val=0, max_val=E - 1)
            e_last = dve.value_load(slot_expert[0:1, at(s - 1)], min_val=0, max_val=E - 1)
            dve.wait_ge(bias_in, e * 16 + 16)
            glu_bias(s, e % 2)
            rest_of_yT(s - 1)
            rest_of_xT(s + 1)
            activate(s, e % 2)
            keep_out(s - 1, e_last % 2)
        e = dve.value_load(slot_expert[0:1, SLOTS - 1:SLOTS], min_val=0, max_val=E - 1)
        e_last = dve.value_load(slot_expert[0:1, SLOTS - 2:SLOTS - 1], min_val=0, max_val=E - 1)
        glu_bias(SLOTS - 1, e % 2)
        rest_of_yT(SLOTS - 2)
        activate(SLOTS - 1, e % 2)
        keep_out(SLOTS - 2, e_last % 2)
        rest_of_yT(SLOTS - 1)

        def add_low(i):
            dve.scalar_tensor_tensor(out=x2_all[:, i, :], in0=low_row[i], scalar=weight[:, 0, i:i + 1],
                                     in1=x2_all[:, i, :], op0=ALU.mult, op1=ALU.add).then_inc(low_added, 1)

        def add_high(i):
            dve.wait_ge(high_row_in[i], 16)
            dve.wait_ge(low_added, i + 1)
            dve.scalar_tensor_tensor(out=x2_all[:, i, :], in0=high_row[i], scalar=weight[:, 1, i:i + 1],
                                     in1=x2_all[:, i, :], op0=ALU.mult, op1=ALU.add).then_inc(high_added, 1)

        dve.wait_ge(places_known, 1)
        dve.wait_ge(low_rows_in, 16 * NT)
        for i in range(LOW_AHEAD):
            add_low(i)
            if i == LOW_EARLY - 1:
                keep_out(SLOTS - 1, e % 2)
        for i in range(NT):
            add_high(i)
            if i + LOW_AHEAD < NT:
                add_low(i + LOW_AHEAD)

    @block.gpsimd
    def _(pool):
        pool.memset(yo, 0.0).then_inc(zeros_made, 1)

        def load_expert(e):
            pool.dma_start(stage, w_all[at(e), :, :].rearrange("o p n -> p (o n)")).then_inc(w_in, 16)

        def load_bias(e, par):
            pool.dma_start(bias[:, par, :], b_all[at(e), :].to_broadcast([P, BCOLS])).then_inc(bias_in, 16)

        def split_expert(e, par):
            load_bias(e, par)
            pool.wait_ge(w_in, loaded)
            pool.reg_add(loaded, loaded, 16)
            pool.tensor_scalar(w_hi[:, par, :], stage, 1.0, 1.0, ALU.mult, ALU.mult).then_inc(hi_done, 1)
            pool.wait_ge(hi_done, e + 1)
            pool.tensor_tensor(w_lo[:, par, :], stage, w_hi[:, par, :].bitcast(F32), ALU.subtract)\
                .then_inc(split_done, 1)
            pool.wait_ge(bias_in, e * 16 + 16)

        loaded = pool.alloc_register("loaded")
        pool.reg_mov(loaded, 16)
        load_bias(0, 0)
        pool.wait_ge(R.pos_done, 2)
        for q in range(late.n):
            scatter_rows(pool, R, late.lo + q, rows[:, q, :], xs_dram)
        pool.wait_ge(split_done, 1)
        for q in range(2):
            pool.wait_ge(xg_in[q], 16)
        load_expert(1)
        split_expert(1, 1)
        with pool.Fori(1, E // 2) as j:
            for q in range(2):
                e = j * 2 + q
                pool.wait_ge(split_done, e)
                load_expert(e)
                end = pool.value_load(ends_i[0:1, at(e - 2)], min_val=1, max_val=SLOTS)
                pool.wait_ge(yo_done, end + PRIME)
                split_expert(e, q)
        end = pool.value_load(ends_i[0:1, E - 2:E - 1], min_val=1, max_val=SLOTS)
        pool.wait_ge(ys_out, end * 16 + 16)
        pool.sem_inc(low_rows_out, 1)
        pool.wait_ge(low_rows_out, 1)
        pool.wait_ge(places_known, 1)
        pool.wait_ge(split_done, E)
        for i in range(NT):
            pool.indirect_dma_start(out=low_row[i], out_offset=None, in_=ys_dram,
                                    in_offset=bass.IndirectOffsetOnAxis(ap=pos_y[:, 0, i:i + 1], axis=0))\
                .then_inc(low_rows_in, 16)
        pool.wait_ge(ys_out, 16 * SLOTS + 16)
        for i in range(NT):
            if i >= len(free_row):
                pool.wait_ge(low_added, i - len(free_row) + 1)
            pool.indirect_dma_start(out=high_row[i], out_offset=None, in_=ys_dram,
                                    in_offset=bass.IndirectOffsetOnAxis(ap=pos_y[:, 1, i:i + 1], axis=0))\
                .then_inc(high_row_in[i], 16)



def build(nc, x, ctxT, inT, chan, xprojT, dtT, g_x, w_all, b_all, gate_wT, gate_b, g_ffn, consts, out):
    with ExitStack() as whole:
        x2_all = whole.enter_context(nc.sbuf_tensor("x2_all", [P, NT, H], F32))
        bc_dram = nc.dram_tensor("bc_dram", [B, 2 * DS, L], F32, kind="Internal").ap()
        xs_dram = nc.dram_tensor("xs_dram", [E * REGION, H], F32, kind="Internal").ap()
        ys_dram = nc.dram_tensor("ys_dram", [SLOTS * P, H], F32, kind="Internal").ap()
        R = routing_buffers(nc, whole)
        shared = whole.enter_context(nc.sbuf_tensor("shared", [P, 4 * HALF * L], F32))
        with ExitStack() as ctx:
            mamba_block(nc, ctx, R, shared, x2_all, x, ctxT, inT, chan, xprojT, dtT, consts, gate_wT, gate_b, g_x,
                        bc_dram, xs_dram, ys_dram, w_all)
        with ExitStack() as ctx:
            moe_block(nc, ctx, R, shared, x2_all, out.rearrange("b l d -> (b l) d"), w_all, b_all, g_ffn, xs_dram, ys_dram)


def kernel(**inputs):
    from concourse import bacc
    from concourse.bass_utils import run_bass_kernel_spmd

    a = {k: np.asarray(v) for k, v in inputs.items()}

    def rows(w, chunks):
        return w.reshape(chunks, P, -1).transpose(1, 0, 2)

    chan = np.concatenate([rows(a["L0_xattn_" + n], ET) for n in ("conv_w", "conv_b", "D", "dt_proj_b", "A_log")], 2)
    w1 = a["L0_ffn_w1"].reshape(E, I, 2, H).transpose(0, 3, 2, 1).reshape(E, HC, P, 2 * I)
    w2 = a["L0_ffn_w2"].transpose(0, 2, 1).reshape(E, IC, P, H)
    w_all = np.concatenate([w.transpose(0, 2, 1, 3).reshape(E, P, -1) for w in (w1, w2)], 2)
    b1 = a["L0_ffn_b1"].reshape(E, I, 2).transpose(0, 2, 1).reshape(E, 2 * I)
    consts = np.concatenate([np.eye(P), np.triu(np.ones((P, P)), 1), np.ones((P, P)),
                             *(np.tile(np.arange(E * n) % n > 0, (P, 1)) for n in (EARLY, NT - EARLY)),
                             np.tile(np.arange(SLOTS), (P, 1)), np.tile(E - np.arange(E), (P, 1)),
                             np.tile(np.arange(E) * REGION, (P, 1))], 1).astype(np.float32)
    arrays = {
        "x": a["x"],
        "ctxT": a["ctx_1024"].transpose(0, 2, 1).reshape(B, KC, P, L),
        "inT": rows(a["L0_xattn_in_proj_w"].T, KC),
        "chan": chan,
        "xprojT": rows(a["L0_xattn_x_proj_w"].T, ET),
        "dtT": a["L0_xattn_dt_proj_w"].T,
        "g_x": a["g_xattn"].reshape(1, 1),
        "w_all": w_all,
        "b_all": np.concatenate([b1, a["L0_ffn_b2"]], 1),
        "gate_wT": rows(a["L0_ffn_gate_w"].T, HC),
        "gate_b": a["L0_ffn_gate_b"].reshape(1, E),
        "g_ffn": a["g_ffn"].reshape(1, 1),
        "consts": consts,
    }
    arrays = {k: np.ascontiguousarray(v) for k, v in arrays.items()}
    nc = bacc.Bacc("TRN2", target_bir_lowering=False, num_devices=1)
    args = [nc.dram_tensor(k, v.shape, F32, kind="ExternalInput").ap() for k, v in arrays.items()]
    out = nc.dram_tensor("out", (B, L, H), F32, kind="ExternalOutput").ap()
    build(nc, *args, out)
    got = run_bass_kernel_spmd(nc, [arrays], core_ids=[0])
    return got.results[0]["out"]
```
